# Optimizing a Trainium2 kernel written in Bass

```python
import numpy as np
import jax
import jax.numpy as jnp

def _softmax(x, axis=-1):
    return jax.nn.softmax(x, axis=axis)

def _gelu(x):
    return jax.nn.gelu(x, approximate=True)

def _silu(x):
    return jax.nn.silu(x)

def _sigmoid(x):
    return jax.nn.sigmoid(x)

def _layernorm(x, axis=-1, eps=1e-05):
    m = jnp.mean(x, axis=axis, keepdims=True)
    v = jnp.var(x, axis=axis, keepdims=True)
    return (x - m) / jnp.sqrt(v + eps)

def _scatter_add(tgt, idx, src, axis=0):
    return tgt.at[idx].add(src)

def _segment_sum(src, seg, n):
    return jax.ops.segment_sum(src, seg, n)
kernel_name = 'mk_decoder_preln_d1_seqx_r4_ab0967'

def setup_inputs(seed: int=0):
    np.random.seed(seed)
    _w = jnp.asarray

    def _rec_inputs():
        import jax
        import jax.numpy as jnp
        _rk = jax.random.key(seed)
        x = 7.22e-05 + 1 * jax.random.normal(jax.random.fold_in(_rk, 1), (4, 512, 512), jnp.float32)
        _lenS = 512 - jax.random.randint(jax.random.fold_in(_rk, 7), (4,), 0, max(1, 512 // 4) + 1, jnp.int32)
        _lenS2 = 512 - jax.random.randint(jax.random.fold_in(_rk, 8), (4,), 0, max(1, 512 // 4) + 1, jnp.int32)
        _ctx_1024P = jax.random.normal(jax.random.fold_in(_rk, 11), (4, 16, 256), jnp.float32)
        _ctx_1024c = jax.random.dirichlet(jax.random.fold_in(_rk, 511), 0.3 * jnp.ones((16,), jnp.float32), (4, 512))
        _ctx_1024t = jnp.einsum('bsk,bkd->bsd', _ctx_1024c, _ctx_1024P)
        _ctx_1024t = _ctx_1024t * jax.lax.rsqrt(jnp.mean(jnp.square(_ctx_1024t)) + 1e-12) * 0.953939
        ctx_1024 = 2.81802e-05 + 1.00001 * (_ctx_1024t + 0.3 * jax.random.normal(jax.random.fold_in(_rk, 611), (4, 512, 256), jnp.float32))
        return (x, ctx_1024)
    x, ctx_1024 = _rec_inputs()

    def _L0_attn_setup():
        import jax, jax.numpy as jnp
        import numpy as np
        DIM = 512
        NUM_HEADS = 16
        HEAD_DIM = 128
        key = jax.random.key(seed)
        ks = jax.random.split(key, 9)
        B, S = (2, 512)
        s = lambda fan_in: 1.0 / np.sqrt(fan_in)
        return {'x': jax.random.normal(ks[0], (B, S, DIM), dtype=jnp.float32), 'Wq': jax.random.uniform(ks[1], (DIM, NUM_HEADS * HEAD_DIM), jnp.float32, -s(DIM), s(DIM)), 'bq': jax.random.uniform(ks[2], (NUM_HEADS * HEAD_DIM,), jnp.float32, -s(DIM), s(DIM)), 'Wk': jax.random.uniform(ks[3], (DIM, HEAD_DIM), jnp.float32, -s(DIM), s(DIM)), 'bk': jax.random.uniform(ks[4], (HEAD_DIM,), jnp.float32, -s(DIM), s(DIM)), 'Wv': jax.random.uniform(ks[5], (DIM, HEAD_DIM), jnp.float32, -s(DIM), s(DIM)), 'bv': jax.random.uniform(ks[6], (HEAD_DIM,), jnp.float32, -s(DIM), s(DIM)), 'Wo': jax.random.uniform(ks[7], (NUM_HEADS * HEAD_DIM, DIM), jnp.float32, -s(NUM_HEADS * HEAD_DIM), s(NUM_HEADS * HEAD_DIM)), 'bo': jax.random.uniform(ks[8], (DIM,), jnp.float32, -s(NUM_HEADS * HEAD_DIM), s(NUM_HEADS * HEAD_DIM))}
    _L0_attn_all = _L0_attn_setup()
    _L0_attn_in = {k: v for k, v in _L0_attn_all.items() if k in ('Wq', 'bq', 'Wk', 'bk', 'Wv', 'bv', 'Wo', 'bo')}
    del _L0_attn_all

    def _L0_xattn_setup():
        import jax, jax.numpy as jnp
        import numpy as np
        key = jax.random.key(seed)
        ks = jax.random.split(key, 6)
        B, L, N, C, D = (8, 128, 512, 256, 128)
        return {'teacher_logits': jax.random.normal(ks[0], (B, L, N), dtype=jnp.float32), 'teacher_features': jax.random.normal(ks[1], (B, N, C), dtype=jnp.float32), 'Wq': jax.random.normal(ks[2], (D, C), dtype=jnp.float32) * (1.0 / np.sqrt(C)), 'bq': jnp.zeros((D,), dtype=jnp.float32), 'Wk': jax.random.normal(ks[3], (D, C), dtype=jnp.float32) * (1.0 / np.sqrt(C)), 'bk': jnp.zeros((D,), dtype=jnp.float32)}
    _L0_xattn_all = _L0_xattn_setup()
    _L0_xattn_in = {k: v for k, v in _L0_xattn_all.items() if k in ('Wq', 'bq', 'Wk', 'bk')}
    del _L0_xattn_all

    def _L0_ffn_setup():
        import jax, jax.numpy as jnp
        import numpy as np
        BLOCK_SIZE = 32
        HIDDEN_SIZE = 512
        MLP_DIM = 4096
        NVFP4_LUT = jnp.array([0.0, 0.5, 1.0, 1.5, 2.0, 3.0, 4.0, 6.0, 0.0, -0.5, -1.0, -1.5, -2.0, -3.0, -4.0, -6.0], dtype=jnp.float32)

        def dequant_nvfp4(W_packed, scales, block=BLOCK_SIZE):
            N = W_packed.shape[0]
            low = W_packed & 15
            high = W_packed >> 4 & 15
            idx = jnp.stack([low, high], axis=-1).reshape(N, -1)
            vals = NVFP4_LUT[idx]
            K = vals.shape[1]
            vals = vals.reshape(N, K // block, block) * scales[:, :, None]
            return vals.reshape(N, K)
        key = jax.random.key(seed)
        ks = jax.random.split(key, 7)
        x = jax.random.normal(ks[0], (4, 32, HIDDEN_SIZE), dtype=jnp.float32)
        gate_W_packed = jax.random.randint(ks[1], (MLP_DIM, HIDDEN_SIZE // 2), 0, 64, dtype=jnp.int32)
        gate_scales = jax.random.uniform(ks[2], (MLP_DIM, HIDDEN_SIZE // BLOCK_SIZE), dtype=jnp.float32) * 0.1 + 0.001
        up_W_packed = jax.random.randint(ks[3], (MLP_DIM, HIDDEN_SIZE // 2), 0, 64, dtype=jnp.int32)
        up_scales = jax.random.uniform(ks[4], (MLP_DIM, HIDDEN_SIZE // BLOCK_SIZE), dtype=jnp.float32) * 0.1 + 0.001
        down_W_packed = jax.random.randint(ks[5], (HIDDEN_SIZE, MLP_DIM // 2), 0, 64, dtype=jnp.int32)
        down_scales = jax.random.uniform(ks[6], (HIDDEN_SIZE, MLP_DIM // BLOCK_SIZE), dtype=jnp.float32) * 0.1 + 0.001
        return {'x': x, 'gate_W_packed': gate_W_packed, 'gate_scales': gate_scales, 'up_W_packed': up_W_packed, 'up_scales': up_scales, 'down_W_packed': down_W_packed, 'down_scales': down_scales}
    _L0_ffn_all = _L0_ffn_setup()
    _L0_ffn_in = {k: v for k, v in _L0_ffn_all.items() if k in ('gate_W_packed', 'gate_scales', 'up_W_packed', 'up_scales', 'down_W_packed', 'down_scales')}
    del _L0_ffn_all
    return {'x': x, 'ctx_1024': ctx_1024, 'L0_attn_Wq': _L0_attn_in['Wq'], 'L0_attn_bq': _L0_attn_in['bq'], 'L0_attn_Wk': _L0_attn_in['Wk'], 'L0_attn_bk': _L0_attn_in['bk'], 'L0_attn_Wv': _L0_attn_in['Wv'], 'L0_attn_bv': _L0_attn_in['bv'], 'L0_attn_Wo': _L0_attn_in['Wo'], 'L0_attn_bo': _L0_attn_in['bo'], 'L0_xattn_Wq': _L0_xattn_in['Wq'], 'L0_xattn_bq': _L0_xattn_in['bq'], 'L0_xattn_Wk': _L0_xattn_in['Wk'], 'L0_xattn_bk': _L0_xattn_in['bk'], 'L0_ffn_gate_W_packed': _L0_ffn_in['gate_W_packed'], 'L0_ffn_gate_scales': _L0_ffn_in['gate_scales'], 'L0_ffn_up_W_packed': _L0_ffn_in['up_W_packed'], 'L0_ffn_up_scales': _L0_ffn_in['up_scales'], 'L0_ffn_down_W_packed': _L0_ffn_in['down_W_packed'], 'L0_ffn_down_scales': _L0_ffn_in['down_scales']}

def reference(x, ctx_1024, L0_attn_Wq, L0_attn_bq, L0_attn_Wk, L0_attn_bk, L0_attn_Wv, L0_attn_bv, L0_attn_Wo, L0_attn_bo, L0_xattn_Wq, L0_xattn_bq, L0_xattn_Wk, L0_xattn_bk, L0_ffn_gate_W_packed, L0_ffn_gate_scales, L0_ffn_up_W_packed, L0_ffn_up_scales, L0_ffn_down_W_packed, L0_ffn_down_scales):
    import jax
    import jax.numpy as jnp

    def _L0_attn_ref(x, Wq, bq, Wk, bk, Wv, bv, Wo, bo):
        import jax, jax.numpy as jnp
        import numpy as np
        DIM = 512
        NUM_HEADS = 16
        HEAD_DIM = 128
        B, S, _ = x.shape
        H, D = (NUM_HEADS, HEAD_DIM)
        q = (x @ Wq + bq).reshape(B, S, H, D)
        k = x @ Wk + bk
        v = x @ Wv + bv
        scale = 1.0 / np.sqrt(D).astype(np.float32)
        scores = jnp.einsum('bnhd,bmd->bnhm', q, k) * scale
        attn = jax.nn.softmax(scores, axis=-1)
        out = jnp.einsum('bnhm,bmd->bnhd', attn, v)
        out = out.reshape(B, S, H * D)
        return out @ Wo + bo

    def _L0_xattn_ref(teacher_logits, teacher_features, Wq, bq, Wk, bk):
        import jax, jax.numpy as jnp
        import numpy as np
        query = jnp.einsum('bnc,dc->bnd', teacher_features, Wq) + bq
        key = jnp.einsum('bnc,dc->bnd', teacher_features, Wk) + bk
        energy = jnp.einsum('bnd,bmd->bnm', query, key)
        attention = jax.nn.softmax(energy, axis=-1)
        x_m = jnp.einsum('bln,bmn->blm', teacher_logits, attention)
        return x_m

    def _L0_ffn_ref(x, gate_W_packed, gate_scales, up_W_packed, up_scales, down_W_packed, down_scales):
        import jax, jax.numpy as jnp
        import numpy as np
        BLOCK_SIZE = 32
        HIDDEN_SIZE = 512
        MLP_DIM = 4096
        NVFP4_LUT = jnp.array([0.0, 0.5, 1.0, 1.5, 2.0, 3.0, 4.0, 6.0, 0.0, -0.5, -1.0, -1.5, -2.0, -3.0, -4.0, -6.0], dtype=jnp.float32)

        def dequant_nvfp4(W_packed, scales, block=BLOCK_SIZE):
            N = W_packed.shape[0]
            low = W_packed & 15
            high = W_packed >> 4 & 15
            idx = jnp.stack([low, high], axis=-1).reshape(N, -1)
            vals = NVFP4_LUT[idx]
            K = vals.shape[1]
            vals = vals.reshape(N, K // block, block) * scales[:, :, None]
            return vals.reshape(N, K)
        B, S, H = x.shape
        xt = x.reshape(B * S, H)
        Wg = dequant_nvfp4(gate_W_packed, gate_scales)
        Wu = dequant_nvfp4(up_W_packed, up_scales)
        Wd = dequant_nvfp4(down_W_packed, down_scales)
        gate = jnp.einsum('th,nh->tn', xt, Wg)
        up = jnp.einsum('th,nh->tn', xt, Wu)
        gelu = jnp.tanh(0.7978845608028654 * (gate + 0.044715 * gate ** 3)) * gate * 0.5 + gate * 0.5
        inter = gelu * up
        out = jnp.einsum('tn,hn->th', inter, Wd)
        return out.reshape(B, S, H)
    x = x + _L0_attn_ref(_layernorm(x, axis=-1), L0_attn_Wq, L0_attn_bq, L0_attn_Wk, L0_attn_bk, L0_attn_Wv, L0_attn_bv, L0_attn_Wo, L0_attn_bo)
    x = x + _L0_xattn_ref(_layernorm(x, axis=-1), ctx_1024, L0_xattn_Wq, L0_xattn_bq, L0_xattn_Wk, L0_xattn_bk)
    x = x + _L0_ffn_ref(_layernorm(x, axis=-1), L0_ffn_gate_W_packed, L0_ffn_gate_scales, L0_ffn_up_W_packed, L0_ffn_up_scales, L0_ffn_down_W_packed, L0_ffn_down_scales)
    return x

_drawn_inputs = setup_inputs


def setup_inputs(seed=0):
    import zlib

    import numpy as np

    out = dict(_drawn_inputs(seed))
    spreads = {'L0_xattn_bq': (0.0, 0.1), 'L0_xattn_bk': (0.0, 0.8)}
    factors = {'L0_attn_Wq': 6.226,
     'L0_attn_bq': 8.0,
     'L0_attn_Wk': 6.213,
     'L0_attn_bk': 8.0,
     'L0_attn_bv': 2.975,
     'L0_attn_bo': 3.181}
    for name, (base, spread) in spreads.items():
        noise = np.random.default_rng([zlib.crc32(name.encode()), seed]).standard_normal(out[name].shape)
        drawn = base * np.exp(spread * noise) if base else spread * noise
        out[name] = jnp.asarray(drawn.astype(out[name].dtype))
    for name, factor in factors.items():
        out[name] = (out[name] * factor).astype(out[name].dtype)
    return out
```

```python
from contextlib import ExitStack

import numpy as np

import concourse.bass as bass
from concourse import mybir

F32 = mybir.dt.float32
F32R = mybir.dt.float32r
I32 = mybir.dt.int32
ACT = mybir.ActivationFunctionType
ALU = mybir.AluOpType
AX = mybir.AxisListType

P = 128
EPS = 1e-5


def decoder_layer(nc, x_in, ctx_in, wq_in, bq_in, wk_in, bk_in, wv_in, bv_in, wo_in, bo_in, xwq_in, xbq_in, xwk_in,
                  xbk_in, gate_in, gate_s_in, up_in, up_s_in, down_in, down_s_in, out):
    B, S, D = x_in.shape
    C = ctx_in.shape[2]
    HD = wk_in.shape[1]
    H = wq_in.shape[1] // HD
    F = gate_in.shape[0]
    NT = S // P
    KC = D // P
    CC = C // P
    SCALE = float(1.0 / np.sqrt(np.float32(HD)))
    assert HD == P and S == 512 and D == S and NT == 4 and KC == 4 and H % 2 == 0

    TILES = (H + 1) * NT
    XH = H
    LN1, CTX, KEY, VAL, XQ, XK, LN2 = 0, 4, 6, 7, 8, 9, 10
    ITEMS = 14
    LAST = H + 3
    LOOP0, LOOP1 = 4, H - 2

    NG = 256
    NCH = NG // P
    G = F // NG
    STEPS = G * B
    UNITS = 3 * NCH
    UNITS_AT = [[0, 2], [1, 3], [4], [5]]
    ORDER = [u for at in UNITS_AT for u in at]
    BLK = 32
    assert G % 2 == 0 and B == 4

    def tiles_before(b, h, j=0):
        return b * TILES + h * NT + j

    ctx = ExitStack()
    with ctx:
        def sem(name):
            return ctx.enter_context(nc.semaphore(name))

        def keep(name, shape, dt=F32):
            return ctx.enter_context(nc.sbuf_tensor(name, shape, dt))

        psum = [ctx.enter_context(nc.psum_tensor(f"bank{n}", [P, 512], F32)) for n in range(8)]
        acc = psum[0:4]
        ps_s, ps_t, ps_q, ps_v = psum[4:8]
        xm_bank = psum[4:8]

        x = keep("x", [P, B * NT, D])
        ident = keep("ident", [P, P])
        neg_half = keep("neg_half", [P, NT])
        stats = keep("stats", [P, NT, 6])
        mv = keep("mv", [P, NT, 2])
        ve = keep("ve", [P, NT])
        rstd = keep("rstd", [P, NT])
        hn = keep("hn", [P, NT, D])

        x_loaded = sem("x_loaded")
        small_loaded = sem("small_loaded")
        ctx_loaded = sem("ctx_loaded")
        wq_loaded = [sem(f"wq_loaded{n}") for n in range(2)]
        wo_loaded = [sem(f"wo_loaded{n}") for n in range(2)]
        packed_loaded = [sem(f"packed_loaded{n}") for n in range(2)]
        scales_loaded = sem("scales_loaded")
        const_made = sem("const_made")
        once_mm = sem("once_mm")
        once_hi = sem("once_hi")
        once_lo = sem("once_lo")
        ln_bn = sem("ln_bn")
        ln_mv = sem("ln_mv")
        ln_ve = sem("ln_ve")
        ln_rstd = sem("ln_rstd")
        h_ready = sem("h_ready")
        bo_added = sem("bo_added")
        held = sem("held")
        item_mm = sem("item_mm")
        item_pre = sem("item_pre")
        item_hi = sem("item_hi")
        item_lo = sem("item_lo")
        wq_hi_made = sem("wq_hi_made")
        wq_lo_made = sem("wq_lo_made")
        wo_hi_made = sem("wo_hi_made")
        wo_lo_made = sem("wo_lo_made")
        q_mm = sem("q_mm")
        q_hi_made = sem("q_hi_made")
        q_lo_made = sem("q_lo_made")
        s_mm = sem("s_mm")
        max_made = sem("max_made")
        exp_made = sem("exp_made")
        rsum_inv = sem("rsum_inv")
        p_normed = sem("p_normed")
        t_mm = sem("t_mm")
        pt_hi_made = sem("pt_hi_made")
        pt_lo_made = sem("pt_lo_made")
        pv_mm = sem("pv_mm")
        at_hi_made = sem("at_hi_made")
        at_lo_made = sem("at_lo_made")
        wo_mm = sem("wo_mm")
        acc_ready = sem("acc_ready")
        att_added = sem("att_added")
        xm_mm = sem("xm_mm")
        xm_added = sem("xm_added")
        scales_times4 = sem("scales_times4")
        dq_shift = sem("dq_shift")
        dq_bits = sem("dq_bits")
        dq_sign = sem("dq_sign")
        dq_clamp = sem("dq_clamp")
        dq_sum = sem("dq_sum")
        dq_value = sem("dq_value")
        dq_weight = sem("dq_weight")
        w_mm = sem("w_mm")
        w_hi_made = sem("w_hi_made")
        w_lo_made = sem("w_lo_made")
        gu_mm = sem("gu_mm")
        sq_made = sem("sq_made")
        z_made = sem("z_made")
        tanh_made = sem("tanh_made")
        a_made = sem("a_made")
        v_made = sem("v_made")
        in_hi_made = sem("in_hi_made")
        in_lo_made = sem("in_lo_made")
        down_mm = sem("down_mm")
        down_added = sem("down_added")
        stored = sem("stored")

        def mm3(pe, bank, w, m, start, stop):
            pe.matmul(bank, w[0], m[0], start=start, stop=False, skip_group_check=True)
            pe.matmul(bank, w[0], m[1], start=False, stop=False, skip_group_check=True)
            return pe.matmul(bank, w[1], m[0], start=False, stop=stop, skip_group_check=True)

        START = 1
        pe_started = (item_mm, xm_mm, pv_mm, wo_mm, s_mm, t_mm, q_mm, w_mm, down_mm)
        act_started = (item_hi, wq_hi_made, wo_hi_made, q_hi_made, at_hi_made, pt_hi_made, exp_made)
        dve_started = (item_lo, item_pre, xm_added, q_lo_made, at_lo_made, pt_lo_made, max_made, p_normed, dq_shift,
                       dq_value, w_lo_made, v_made, in_lo_made, h_ready)
        pool_started = (wq_lo_made, wo_lo_made, dq_sum, dq_weight)

        def start(engine, sems):
            for s in sems:
                engine.sem_inc(s, START)

        def at_least_0(n):
            return max(n, 0) if isinstance(n, int) else n

        def hold(engine):
            engine.sem_inc(held, 1)

        def f32(ap):
            return ap.bitcast(F32)

        def layer_norm_stats(dve, n, xt):
            for t in range(NT):
                dve.bn_stats(stats[:, t, :], xt(t)).then_inc(ln_bn, 1)
            dve.wait_ge(ln_bn, n * NT + NT)
            hold(dve)
            for t in range(NT):
                dve.bn_aggr(mv[:, t, :], stats[:, t, :]).then_inc(ln_mv, 1)

        def layer_norm_scale(dve, n, xt):
            dve.wait_ge(ln_rstd, n + 1)
            for t in range(NT):
                dve.tensor_scalar(hn[:, t, :], xt(t), mv[:, t, 0:1], rstd[:, t:t + 1], ALU.subtract,
                                  ALU.mult).then_inc(h_ready, 1)

        def layer_norm_rstd(pool, n):
            pool.wait_ge(ln_mv, n * NT + NT)
            hold(pool)
            pool.tensor_scalar(ve[:], mv[:, :, 1], EPS, None, ALU.add).then_inc(ln_ve, 1)
            pool.wait_ge(ln_ve, n + 1)
            pool.tensor_tensor(rstd[:], ve[:], neg_half[:], ALU.pow).then_inc(ln_rstd, 1)

        with ExitStack() as att:
            def sb(name, shape, dt=F32):
                return att.enter_context(nc.sbuf_tensor(name, shape, dt))

            def pair(name, shape):
                return sb(name + "_hi", shape, F32R), sb(name + "_lo", shape, F32R)

            hT = pair("hT", [P, KC, S])
            kT = pair("kT", [P, S])
            v = pair("v", [P, NT, HD])
            kf = sb("kf", [P, S])
            vf = sb("vf", [P, NT, HD])
            wkv = sb("wkv", [P, 2, KC, HD])
            wkv_p = pair("wkv", [P, 2, KC, HD])
            bq = sb("bq", [P, H])
            bk = sb("bk", [P, 1])
            bv = sb("bv", [P, HD])
            bo = sb("bo", [P, D])
            xbq = sb("xbq", [P, 1])
            xbk = sb("xbk", [P, 1])
            xw = sb("xw", [P, 2, C])
            xwT = pair("xwT", [P, 2, CC, HD])
            ctx_sb = sb("ctx_sb", [P, NT, C])
            ctxT = pair("ctxT", [P, CC, S])
            xq = pair("xq", [P, S])
            xk = pair("xk", [P, S])
            zeros = sb("zeros", [P, S], F32R)
            wq_st = sb("wq_st", [P, 2, KC, HD])
            wo_st = sb("wo_st", [P, 2, D])
            wq = [pair(f"wq{n}", [P, KC, HD]) for n in range(2)]
            wo = [pair(f"wo{n}", [P, D]) for n in range(2)]
            q = [pair(f"q{n}", [P, S]) for n in range(2)]
            prob = sb("prob", [P, 2, NT, S])
            neg_max = sb("neg_max", [P, 2, NT])
            rsum = sb("rsum", [P, 2, NT])
            rinv = sb("rinv", [P, 2, NT])
            pT = [pair(f"pT{n}", [P, NT, S]) for n in range(2)]
            at = [pair(f"at{n}", [P, S]) for n in range(2)]

            wq_dram = wq_in.rearrange("(c p) (h d) -> p c h d", p=P, d=HD)
            wo_dram = wo_in.rearrange("(h d) n -> d h n", d=HD)
            ctx_dram = ctx_in.rearrange("b (t p) c -> b p t c", p=P)
            x_dram = x_in.rearrange("b (t p) n -> b p t n", p=P)
            SMALL_LOADS = 11

            def at_work(i, lag, n):
                return not isinstance(i, int) or 0 <= i - lag < n

            def before(b, per, h, less):
                return b * per + at_least_0(h - less)

            def pipeline(engine, b, iteration, first, last):
                for i in range(first, LOOP0):
                    iteration(b, i, i % 2)
                with engine.Fori(0, (LOOP1 - LOOP0) // 2) as n:
                    for par in range(2):
                        iteration(b, n * 2 + (LOOP0 + par), par)
                for i in range(LOOP1, last + 1):
                    iteration(b, i, i % 2)

            blk = att.enter_context(nc.Block())

            @blk.sync
            def _(sp):
                for b in range(B):
                    sp.dma_start(x[:, b * NT:(b + 1) * NT, :], x_dram[b]).then_inc(x_loaded, 16)
                    if b == 0:
                        with nc.allow_non_contiguous_dma(reason="biases as columns, once"):
                            for dst, src in (
                                (wkv[:, 0], wk_in.rearrange("(c p) d -> p c d", p=P)),
                                (wkv[:, 1], wv_in.rearrange("(c p) d -> p c d", p=P)),
                                (xw[:, 0, :], xwq_in), (xw[:, 1, :], xwk_in),
                                (bk[:], bk_in.rearrange("(p a) -> p a", a=1)),
                                (xbq[:], xbq_in.rearrange("(p a) -> p a", a=1)),
                                (xbk[:], xbk_in.rearrange("(p a) -> p a", a=1)),
                                (bv[:], bv_in.partition_broadcast(P)),
                                (bo[:], bo_in.partition_broadcast(P)),
                            ):
                                sp.dma_start(dst, src).then_inc(small_loaded, 16)
                            sp.dma_start(bq[:, 0:H // 2], bq_in.rearrange("(h d) -> d h", d=HD)[:, 0:H // 2])\
                              .then_inc(small_loaded, 16)
                            sp.dma_start(bq[:, H // 2:H], bq_in.rearrange("(h d) -> d h", d=HD)[:, H // 2:H])\
                              .then_inc(small_loaded, 16)

                def iteration(b, i, par):
                    if at_work(i, -2, H):
                        sp.wait_ge(wq_lo_made, START + before(b, H, i + 2, 1))
                        sp.dma_start(wq_st[:, par], wq_dram[:, :, i + 2, :]).then_inc(wq_loaded[par], 16)
                    if at_work(i, 1, H):
                        sp.wait_ge(wo_lo_made, START + before(b, H, i - 1, 1))
                        sp.dma_start(wo_st[:, 1 - par], wo_dram[:, i - 1, :]).then_inc(wo_loaded[1 - par], 16)

                with sp.Fori(0, B) as b:
                    sp.wait_ge(item_mm, START + b * ITEMS)
                    sp.dma_start(ctx_sb[:], ctx_dram[b]).then_inc(ctx_loaded, 16)
                    pipeline(sp, b, iteration, -2, H)

            @blk.gpsimd
            def _(pool):
                start(pool, pool_started)
                pool.memset(ident[:], 0.0).then_inc(const_made, 1)
                pool.wait_ge(const_made, 1)
                pool.affine_select(out=ident[:], in_=ident[:], compare_op=ALU.not_equal, fill=1.0, base=0,
                                   pattern=[[-1, P]], channel_multiplier=1).then_inc(const_made, 1)
                pool.memset(neg_half[:], -0.5).then_inc(const_made, 1)
                pool.wait_ge(const_made, 3)

                def iteration(b, i, par):
                    if at_work(i, -1, H):
                        h = i + 1
                        w = wq[1 - par]
                        pool.wait_ge(wq_hi_made, START + b * H + h + 1)
                        pool.tensor_tensor(w[1][:], wq_st[:, 1 - par], f32(w[0][:]), ALU.subtract)\
                            .then_inc(wq_lo_made, 1)
                    if at_work(i, 3, H):
                        h = i - 3
                        w = wo[1 - par]
                        pool.wait_ge(wo_hi_made, START + b * H + h + 1)
                        pool.tensor_tensor(w[1][:], wo_st[:, 1 - par], f32(w[0][:]), ALU.subtract)\
                            .then_inc(wo_lo_made, 1)

                with pool.Fori(0, B) as b:
                    layer_norm_rstd(pool, b * 2)
                    for t in range(NT):
                        if t == 0:
                            pool.wait_ge(small_loaded, 16 * SMALL_LOADS)
                        pool.wait_ge(h_ready, START + b * 2 * NT + t + 1)
                        pool.tensor_tensor(x[:, b * NT + t, :], x[:, b * NT + t, :], bo[:], ALU.add)\
                            .then_inc(bo_added, 1)
                    pipeline(pool, b, iteration, -1, LAST)
                    layer_norm_rstd(pool, b * 2 + 1)

            @blk.tensor
            def _(pe):
                start(pe, pe_started)
                pe.wait_ge(const_made, 3)
                pe.wait_ge(small_loaded, 16 * SMALL_LOADS)
                for n in range(2):
                    for c in range(CC):
                        mm = pe.transpose(ps_v[:, (n * CC + c) * P:(n * CC + c + 1) * P],
                                          xw[:, n, c * P:(c + 1) * P], ident[:])
                mm.then_inc(once_mm, 1)
                pe.wait_ge(once_lo, 3)

                def transposed_tile(bank, t):
                    for c in range(KC):
                        mm = pe.transpose(bank[:, c * P:(c + 1) * P], hn[:, t, c * P:(c + 1) * P], ident[:])
                    mm.then_inc(item_mm, 1)

                def iteration(b, i, par):
                    for j in range(NT):
                        if at_work(i, 2, H + 1):
                            h, p = i - 2, par
                            pe.wait_ge(p_normed, START + tiles_before(b, h, j + 1))
                            pe.wait_ge(pt_lo_made, START + tiles_before(b, h, j))
                            for c in range(NT):
                                mm = pe.transpose(ps_t[:, c * P:(c + 1) * P], prob[:, p, j, c * P:(c + 1) * P],
                                                  ident[:])
                            mm.then_inc(t_mm, 1)
                        if at_work(i, 3, H):
                            h, p = i - 3, 1 - par
                            if j == 0:
                                pe.wait_ge(pt_lo_made, START + tiles_before(b, h, NT))
                                pe.wait_ge(at_lo_made, START + b * H + h)
                            mm = mm3(pe, ps_v[:], (v[0][:, j, :], v[1][:, j, :]),
                                     (pT[p][0][:, j, :], pT[p][1][:, j, :]), j == 0, j == NT - 1)
                            if j == NT - 1:
                                mm.then_inc(pv_mm, 1)
                        if at_work(i, 0, H):
                            if j == 0:
                                pe.wait_ge(wq_lo_made, START + b * H + i + 1)
                                pe.wait_ge(q_lo_made, START + b * H + i)
                            w = wq[par]
                            mm = mm3(pe, ps_q[:], (w[0][:, j, :], w[1][:, j, :]), (hT[0][:, j, :], hT[1][:, j, :]),
                                     j == 0, j == KC - 1)
                            if j == KC - 1:
                                mm.then_inc(q_mm, 1)
                        if at_work(i, 1, H + 1):
                            h, p = i - 1, 1 - par
                            cross = isinstance(i, int) and h == XH
                            if j == 0 and not cross:
                                pe.wait_ge(q_lo_made, START + b * H + h + 1)
                            pe.wait_ge(exp_made, START + tiles_before(b, h, j))
                            qq, kk = (xq, xk) if cross else (q[p], kT)
                            mm3(pe, ps_s[:], (qq[0][:, j * P:(j + 1) * P], qq[1][:, j * P:(j + 1) * P]),
                                (kk[0][:], kk[1][:]), True, True).then_inc(s_mm, 1)
                        if at_work(i, 4, H):
                            h, p = i - 4, par
                            if j == 0:
                                pe.wait_ge(wo_lo_made, START + b * H + h + 1)
                                pe.wait_ge(at_lo_made, START + b * H + h + 1)
                            last = isinstance(i, int) and h == H - 1
                            mm = mm3(pe, acc[j][:], (at[p][0][:, j * P:(j + 1) * P], at[p][1][:, j * P:(j + 1) * P]),
                                     (wo[p][0][:], wo[p][1][:]), False, last)
                            if last:
                                mm.then_inc(acc_ready, 1)
                            elif j == NT - 1:
                                mm.then_inc(wo_mm, 1)
                    if isinstance(i, int) and i - 4 == H - 1:
                        pe.matmul(ps_v[:], zeros[:, 0:P], zeros[:], start=True, stop=True,
                                  skip_group_check=True).then_inc(wo_mm, 1)

                with pe.Fori(0, B) as b:
                    pe.wait_ge(item_lo, START + b * ITEMS)
                    for t in range(NT):
                        pe.wait_ge(h_ready, START + b * 2 * NT + t + 1)
                        transposed_tile(acc[t], t)
                    pe.wait_ge(ctx_loaded, b * 16 + 16)
                    pe.wait_ge(xm_added, START + b * NT)
                    for n, bank in enumerate((ps_s, ps_t)):
                        for m in range(2):
                            for c in range(CC):
                                mm = pe.transpose(bank[:, (m * CC + c) * P:(m * CC + c + 1) * P],
                                                  ctx_sb[:, 2 * n + m, c * P:(c + 1) * P], ident[:])
                        mm.then_inc(item_mm, 1)
                    pe.wait_ge(item_lo, START + b * ITEMS + LN1 + NT)
                    for c in range(KC):
                        mm = mm3(pe, ps_q[:], (wkv_p[0][:, 0, c, :], wkv_p[1][:, 0, c, :]),
                                 (hT[0][:, c, :], hT[1][:, c, :]), c == 0, c == KC - 1)
                    mm.then_inc(item_mm, 1)
                    for t in range(NT):
                        for c in range(KC):
                            mm = mm3(pe, ps_v[:, t * P:(t + 1) * P],
                                     (hT[0][:, c, t * P:(t + 1) * P], hT[1][:, c, t * P:(t + 1) * P]),
                                     (wkv_p[0][:, 1, c, :], wkv_p[1][:, 1, c, :]), c == 0, c == KC - 1)
                    mm.then_inc(item_mm, 1)
                    pe.wait_ge(item_lo, START + b * ITEMS + CTX + 2)
                    for n, bank in enumerate((ps_s, ps_t)):
                        for c in range(CC):
                            mm = mm3(pe, bank[:], (xwT[0][:, n, c, :], xwT[1][:, n, c, :]),
                                     (ctxT[0][:, c, :], ctxT[1][:, c, :]), c == 0, c == CC - 1)
                        mm.then_inc(item_mm, 1)
                    for t in range(NT):
                        pe.matmul(acc[t][:], zeros[:, 0:P], zeros[:], start=True, stop=False, skip_group_check=True)
                    pe.wait_ge(item_lo, START + b * ITEMS + XK + 1)
                    pipeline(pe, b, iteration, 0, LAST)
                    for t in range(NT):
                        pe.wait_ge(h_ready, START + (b * 2 + 1) * NT + t + 1)
                        transposed_tile(acc[t], t)
                    pe.wait_ge(pt_lo_made, START + tiles_before(b + 1, 0))
                    pe.wait_ge(q_lo_made, START + b * H + H)
                    pe.wait_ge(at_lo_made, START + b * H + H)
                    pe.wait_ge(item_lo, START + b * ITEMS + ITEMS)
                    for t in range(NT):
                        for c in range(KC):
                            mm = mm3(pe, xm_bank[t][:],
                                     (hT[0][:, c, t * P:(t + 1) * P], hT[1][:, c, t * P:(t + 1) * P]),
                                     (pT[XH % 2][0][:, c, :], pT[XH % 2][1][:, c, :]), c == 0, c == KC - 1)
                        mm.then_inc(xm_mm, 1)

            @blk.scalar
            def _(act):
                start(act, act_started)
                act.wait_ge(small_loaded, 16 * SMALL_LOADS)
                act.activation(wkv_p[0][:], wkv[:], ACT.Copy).then_inc(once_hi, 1)
                act.wait_ge(once_mm, 1)
                act.activation(xwT[0][:].rearrange("p a c d -> p (a c d)"), ps_v[:], ACT.Copy).then_inc(once_hi, 1)

                def tile_hi(b, n, t):
                    act.wait_ge(item_mm, START + b * ITEMS + n + t + 1)
                    act.activation(hT[0][:, :, t * P:(t + 1) * P], acc[t][:].rearrange("p (c n) -> p c n", c=KC),
                                   ACT.Copy).then_inc(item_hi, 1)

                def iteration(b, i, par):
                    for j in range(NT):
                        if at_work(i, 2, H + 1):
                            h, p = i - 2, par
                            act.wait_ge(t_mm, START + tiles_before(b, h, j + 1))
                            if j == 0:
                                act.wait_ge(pv_mm, START + before(b, H, h, 1))
                                if isinstance(h, int) and h == 0:
                                    act.wait_ge(xm_mm, START + b * NT)
                            act.activation(pT[p][0][:, :, j * P:(j + 1) * P],
                                           ps_t[:].rearrange("p (c n) -> p c n", c=NT), ACT.Copy)\
                               .then_inc(pt_hi_made, 1)
                        if j == NT - 1 and at_work(i, 3, H):
                            h, p = i - 3, 1 - par
                            act.wait_ge(pv_mm, START + b * H + h + 1)
                            act.wait_ge(wo_mm, START + before(b, H, h, 1))
                            act.activation(at[p][0][:], ps_v[:], ACT.Copy).then_inc(at_hi_made, 1)
                        if j == NT - 1 and at_work(i, 0, H):
                            act.wait_ge(q_mm, START + b * H + i + 1)
                            act.wait_ge(s_mm, START + b * TILES + at_least_0(i - 1) * NT)
                            act.activation(q[par][0][:], ps_q[:], ACT.Identity, bias=bq[:, bass.ds(i, 1)])\
                               .then_inc(q_hi_made, 1)
                        if at_work(i, 1, H + 1):
                            h, p = i - 1, 1 - par
                            act.wait_ge(max_made, START + tiles_before(b, h, j + 1))
                            act.wait_ge(t_mm, START + b * TILES + (0 if isinstance(h, int) and h < 2 else (h - 2) * NT + j + 1))
                            act.activation(prob[:, p, j, :], ps_s[:], ACT.Exp, bias=neg_max[:, p, j:j + 1],
                                           accum_out=rsum[:, p, j:j + 1]).then_inc(exp_made, 1)
                        if j == 0 and at_work(i, -1, H):
                            h, p = i + 1, 1 - par
                            wait_loaded(wq_loaded[p], b, h, p)
                            act.wait_ge(q_mm, START + before(b, H, h, 1))
                            act.activation(wq[p][0][:], wq_st[:, p], ACT.Copy).then_inc(wq_hi_made, 1)
                        if j == 1 and at_work(i, 3, H):
                            h, p = i - 3, 1 - par
                            wait_loaded(wo_loaded[p], b, h, p)
                            act.wait_ge(wo_mm, START + before(b, H, h, 1))
                            act.activation(wo[p][0][:], wo_st[:, p], ACT.Copy).then_inc(wo_hi_made, 1)

                def wait_loaded(loaded, b, h, p):
                    act.wait_ge(loaded, b * (8 * H) + h * 8 + (16 - 8 * p))

                with act.Fori(0, B) as b:
                    act.wait_ge(xm_mm, START + b * NT)
                    for t in range(NT):
                        tile_hi(b, LN1, t)
                    for n, bank in enumerate((ps_s, ps_t)):
                        act.wait_ge(item_mm, START + b * ITEMS + CTX + n + 1)
                        act.activation(ctxT[0][:, :, 2 * n * P:(2 * n + 2) * P].rearrange("p c (m n) -> p m c n", m=2),
                                       bank[:].rearrange("p (m c n) -> p m c n", m=2, c=CC), ACT.Copy)\
                           .then_inc(item_hi, 1)
                    act.wait_ge(item_pre, START + b * 2 + 1)
                    act.activation(kT[0][:], kf[:], ACT.Copy).then_inc(item_hi, 1)
                    act.wait_ge(item_pre, START + b * 2 + 2)
                    act.activation(v[0][:], vf[:], ACT.Copy).then_inc(item_hi, 1)
                    for n, (bank, dst, bias) in enumerate(((ps_s, xq, xbq), (ps_t, xk, xbk))):
                        act.wait_ge(item_mm, START + b * ITEMS + XQ + n + 1)
                        act.activation(dst[0][:], bank[:], ACT.Identity, bias=bias[:]).then_inc(item_hi, 1)
                    pipeline(act, b, iteration, -1, LAST)
                    for t in range(NT):
                        tile_hi(b, LN2, t)

            @blk.vector
            def _(dve):
                def x_tile(b):
                    return lambda t: x[:, b * NT + t, :]

                def tile_lo(b, n, t):
                    dve.wait_ge(item_hi, START + b * ITEMS + n + t + 1)
                    dve.tensor_tensor(hT[1][:, :, t * P:(t + 1) * P], acc[t][:].rearrange("p (c n) -> p c n", c=KC),
                                      f32(hT[0][:, :, t * P:(t + 1) * P]), ALU.subtract).then_inc(item_lo, 1)

                start(dve, dve_started)
                dve.memset(f32(zeros[:]), 0.0).then_inc(once_lo, 1)
                dve.wait_ge(once_hi, 1)
                dve.tensor_tensor(wkv_p[1][:], wkv[:], f32(wkv_p[0][:]), ALU.subtract).then_inc(once_lo, 1)
                dve.wait_ge(once_hi, 2)
                dve.tensor_tensor(xwT[1][:].rearrange("p a c d -> p (a c d)"), ps_v[:],
                                  f32(xwT[0][:].rearrange("p a c d -> p (a c d)")), ALU.subtract).then_inc(once_lo, 1)
                dve.wait_ge(x_loaded, 16 * B)

                def normalise(b, h, p, j):
                    dve.wait_ge(exp_made, START + tiles_before(b, h, j + 1))
                    dve.reciprocal(rinv[:, p, j:j + 1], rsum[:, p, j:j + 1]).then_inc(rsum_inv, 1)
                    dve.wait_ge(rsum_inv, tiles_before(b, h, j + 1))
                    dve.tensor_scalar(prob[:, p, j, :], prob[:, p, j, :], rinv[:, p, j:j + 1], None, ALU.mult)\
                       .then_inc(p_normed, 1)

                def iteration(b, i, par):
                    for j in range(NT):
                        if j == 0 and at_work(i, 2, H + 1):
                            normalise(b, i - 2, par, NT - 1)
                        if j > 0 and at_work(i, 1, H + 1):
                            normalise(b, i - 1, 1 - par, j - 1)
                        if at_work(i, 2, H + 1):
                            h, p = i - 2, par
                            dve.wait_ge(pt_hi_made, START + tiles_before(b, h, j + 1))
                            dve.tensor_tensor(pT[p][1][:, :, j * P:(j + 1) * P],
                                              ps_t[:].rearrange("p (c n) -> p c n", c=NT),
                                              f32(pT[p][0][:, :, j * P:(j + 1) * P]), ALU.subtract)\
                               .then_inc(pt_lo_made, 1)
                        if j == NT - 1 and at_work(i, 3, H):
                            h, p = i - 3, 1 - par
                            dve.wait_ge(at_hi_made, START + b * H + h + 1)
                            dve.tensor_tensor(at[p][1][:], ps_v[:], f32(at[p][0][:]), ALU.subtract)\
                               .then_inc(at_lo_made, 1)
                        if at_work(i, 1, H + 1):
                            h, p = i - 1, 1 - par
                            dve.wait_ge(s_mm, START + tiles_before(b, h, j + 1))
                            dve.tensor_reduce(neg_max[:, p, j:j + 1], ps_s[:], AX.X, ALU.max, negate=True)\
                               .then_inc(max_made, 1)
                        if j == NT - 1 and at_work(i, 0, H):
                            dve.wait_ge(q_hi_made, START + b * H + i + 1)
                            dve.scalar_tensor_tensor(out=q[par][1][:], in0=ps_q[:], scalar=bq[:, bass.ds(i, 1)],
                                                     in1=f32(q[par][0][:]), op0=ALU.add, op1=ALU.subtract)\
                               .then_inc(q_lo_made, 1)

                with dve.Fori(0, B) as b:
                    layer_norm_stats(dve, b * 2, x_tile(b))
                    dve.wait_ge(item_mm, START + b * ITEMS)
                    layer_norm_scale(dve, b * 2, x_tile(b))
                    for t in range(NT):
                        tile_lo(b, LN1, t)
                    for n, bank in enumerate((ps_s, ps_t)):
                        dve.wait_ge(item_hi, START + b * ITEMS + CTX + n + 1)
                        for m in range(2):
                            ins = dve.tensor_tensor(
                                ctxT[1][:, :, (2 * n + m) * P:(2 * n + m + 1) * P],
                                bank[:, m * CC * P:(m + 1) * CC * P].rearrange("p (c n) -> p c n", c=CC),
                                f32(ctxT[0][:, :, (2 * n + m) * P:(2 * n + m + 1) * P]), ALU.subtract)
                        ins.then_inc(item_lo, 1)
                    dve.wait_ge(item_mm, START + b * ITEMS + KEY + 1)
                    dve.tensor_scalar(kf[:], ps_q[:], bk[:], SCALE, ALU.add, ALU.mult).then_inc(item_pre, 1)
                    dve.wait_ge(item_mm, START + b * ITEMS + VAL + 1)
                    for t in range(NT):
                        ins = dve.tensor_tensor(vf[:, t, :], ps_v[:, t * P:(t + 1) * P], bv[:], ALU.add)
                    ins.then_inc(item_pre, 1)
                    for n, (f, dst) in enumerate(((kf, kT), (vf, v))):
                        dve.wait_ge(item_hi, START + b * ITEMS + KEY + n + 1)
                        dve.tensor_tensor(dst[1][:], f[:], f32(dst[0][:]), ALU.subtract).then_inc(item_lo, 1)
                    for n, (bank, dst, bias) in enumerate(((ps_s, xq, xbq), (ps_t, xk, xbk))):
                        dve.wait_ge(item_hi, START + b * ITEMS + XQ + n + 1)
                        dve.scalar_tensor_tensor(out=dst[1][:], in0=bank[:], scalar=bias[:], in1=f32(dst[0][:]),
                                                 op0=ALU.add, op1=ALU.subtract).then_inc(item_lo, 1)
                    pipeline(dve, b, iteration, 0, LAST)
                    dve.wait_ge(bo_added, b * NT + NT)
                    for t in range(NT):
                        dve.wait_ge(acc_ready, b * NT + t + 1)
                        dve.tensor_tensor(x[:, b * NT + t, :], acc[t][:], x[:, b * NT + t, :], ALU.add)\
                           .then_inc(att_added, 1)
                    dve.wait_ge(att_added, b * NT + NT)
                    hold(dve)
                    layer_norm_stats(dve, b * 2 + 1, x_tile(b))
                    layer_norm_scale(dve, b * 2 + 1, x_tile(b))
                    for t in range(NT):
                        tile_lo(b, LN2, t)
                    for t in range(NT):
                        dve.wait_ge(xm_mm, START + b * NT + t + 1)
                        dve.tensor_tensor(x[:, b * NT + t, :], xm_bank[t][:], x[:, b * NT + t, :], ALU.add)\
                           .then_inc(xm_added, 1)

        with ExitStack() as ffn:
            def sb(name, shape, dt=F32):
                return ffn.enter_context(nc.sbuf_tensor(name, shape, dt))

            def pair(name, shape):
                return sb(name + "_hi", shape, F32R), sb(name + "_lo", shape, F32R)

            h3T = pair("h3T", [P, KC, B * S])
            wg = [pair(f"wg{n}", [P, NCH, KC, P]) for n in range(2)]
            wu = [pair(f"wu{n}", [P, NCH, KC, P]) for n in range(2)]
            wd = [pair(f"wd{n}", [P, NCH, D]) for n in range(2)]
            inter = [pair(f"inter{n}", [P, NCH, S]) for n in range(2)]
            act_buf = [sb(f"act_buf{n}", [P, S]) for n in range(NCH)]
            packed = sb("packed", [P, 3, 512], I32)
            gate_s = sb("gate_s", [P, F // P, D // BLK])
            up_s = sb("up_s", [P, F // P, D // BLK])
            down_s = sb("down_s", [P, KC, F // BLK])
            dq_f = sb("dq_f", [P, 2, 512])
            dq_g = sb("dq_g", [P, 2, 512])
            dq_c = sb("dq_c", [P, 2, 512])
            dq_w = sb("dq_w", [P, 2, 512])

            bank_g, bank_u = psum[0:2], psum[2:4]
            bank_d = psum[4:6]
            bank_w = psum[6:8]

            CODE_MASK = np.int32(np.uint32(0x81C00000).view(np.int32)).item()
            CODE_EXP = 0x3E000000
            gate_dram = gate_in.rearrange("(g n p) k -> p g n k", p=P, n=NCH)
            up_dram = up_in.rearrange("(g n p) k -> p g n k", p=P, n=NCH)
            down_dram = down_in.rearrange("(t p) (g k) -> p g t k", p=P, k=NG // 2)
            out_dram = out.rearrange("b (t p) n -> b p t n", p=P)
            GELU_A, GELU_B = 0.7978845608028654, 0.044715

            blk = ffn.enter_context(nc.Block())

            def unit_index(g, n):
                return g * UNITS + n

            @blk.sync
            def _(sp):
                with nc.allow_non_contiguous_dma(reason="scales"):
                    sp.dma_start(gate_s[:], gate_s_in.rearrange("(n p) k -> p n k", p=P)).then_inc(scales_loaded, 16)
                    sp.dma_start(up_s[:], up_s_in.rearrange("(n p) k -> p n k", p=P)).then_inc(scales_loaded, 16)
                    sp.dma_start(down_s[:], down_s_in.rearrange("(t p) k -> p t k", p=P)).then_inc(scales_loaded, 16)
                with sp.Fori(0, G) as g:
                    sp.wait_ge(dq_shift, START + g * (2 * UNITS))
                    sp.dma_start(packed[:, 0, :].rearrange("p (n k) -> p n k", n=NCH), gate_dram[:, g])\
                      .then_inc(packed_loaded[0], 16)
                    sp.dma_start(packed[:, 1, :].rearrange("p (n k) -> p n k", n=NCH), up_dram[:, g])\
                      .then_inc(packed_loaded[0], 16)
                    sp.dma_start(packed[:, 2, :].rearrange("p (t k) -> p t k", t=KC), down_dram[:, g])\
                      .then_inc(packed_loaded[1], 16)
                for b in range(B):
                    sp.wait_ge(down_added, 2 + (G - 1) * B * NT + (b + 1) * NT)
                    sp.dma_start(out_dram[b], x[:, b * NT:(b + 1) * NT, :]).then_inc(stored, 16)
                sp.wait_ge(stored, 16 * B)

            def substeps(emit, engine):
                with engine.Fori(0, G // 2 - 1) as n:
                    for k in range(2 * B):
                        emit(n * 2 + k // B, k // B, k % B, False)
                for k in range(2 * B):
                    emit(G - 2 + k // B, k // B, k % B, k // B == 1)

            @blk.gpsimd
            def _(pool):
                with pool.Fori(0, B) as b:
                    layer_norm_rstd(pool, b + 2 * B)
                pool.wait_ge(scales_times4, 3)

                def unit(g, n, k):
                    u, r = unit_index(g, n), n % 2
                    pool.wait_ge(dq_clamp, u + 1)
                    pool.tensor_tensor(dq_g[:, r, :], dq_g[:, r, :], dq_f[:, r, :], ALU.add).then_inc(dq_sum, 1)
                    pool.wait_ge(dq_value, START + u + 1)
                    pool.wait_ge(w_mm, START + at_least_0(u - 1))
                    if k < 2 * NCH:
                        sc = (gate_s, up_s)[k // NCH][:, bass.ds(g * NCH + k % NCH, 1), :]\
                            .rearrange("p a k -> p (a k)").unsqueeze(2).to_broadcast([P, D // BLK, BLK])
                        ins = pool.tensor_tensor(dq_w[:, r, :].rearrange("p (k e) -> p k e", e=BLK),
                                                 dq_c[:, r, :].rearrange("p (k e) -> p k e", e=BLK), sc, ALU.mult)
                    else:
                        j = k - 2 * NCH
                        sc = down_s[:, :, bass.ds(g * (NG // BLK) + j * (P // BLK), P // BLK)]\
                            .unsqueeze(3).to_broadcast([P, KC, P // BLK, BLK])
                        ins = pool.tensor_tensor(
                            dq_w[:, r, :].rearrange("p (t k e) -> p t k e", t=KC, e=BLK),
                            dq_c[:, r, :].rearrange("p (t k e) -> p t k e", t=KC, e=BLK), sc, ALU.mult)
                    ins.then_inc(dq_weight, 1)

                for n, k in enumerate(ORDER):
                    unit(0, n, k)

                def emit(g, gp, b, last_group):
                    if not last_group:
                        for k in UNITS_AT[b]:
                            unit(g + 1, ORDER.index(k), k)

                substeps(emit, pool)

            @blk.tensor
            def _(pe):
                with pe.Fori(0, B) as b:
                    for t in range(NT):
                        pe.wait_ge(h_ready, START + (b + 2 * B) * NT + t + 1)
                        pe.wait_ge(item_lo, START + B * ITEMS + b * NT)
                        for c in range(KC):
                            mm = pe.transpose(acc[t][:, c * P:(c + 1) * P], hn[:, t, c * P:(c + 1) * P], ident[:])
                        mm.then_inc(item_mm, 1)

                def unit(g, n):
                    u, r = unit_index(g, n), n % 2
                    pe.wait_ge(dq_weight, START + u + 1)
                    pe.wait_ge(w_lo_made, START + at_least_0(u - 1))
                    for c in range(KC):
                        mm = pe.transpose(bank_w[r][:, c * P:(c + 1) * P], dq_w[:, r, c * P:(c + 1) * P], ident[:])
                    mm.then_inc(w_mm, 1)

                def gate_up(g, gp, b, n):
                    s = g * B + b
                    if b == 0:
                        pe.wait_ge(w_lo_made, START + unit_index(g, 2 * (n + 1)))
                    pe.wait_ge(v_made, START + at_least_0((s - 1) * NCH + n + 1))
                    for w, bank in ((wg[gp], bank_g[n]), (wu[gp], bank_u[n])):
                        for c in range(KC):
                            mm = mm3(pe, bank[:], (w[0][:, n, c, :], w[1][:, n, c, :]),
                                     (h3T[0][:, c, b * S:(b + 1) * S], h3T[1][:, c, b * S:(b + 1) * S]),
                                     c == 0, c == KC - 1)
                        mm.then_inc(gu_mm, 1)

                def down(g, gp, b, t):
                    s = g * B + b
                    if t == 0:
                        pe.wait_ge(in_lo_made, START + s * NCH + NCH)
                        if b == 0:
                            pe.wait_ge(w_lo_made, START + unit_index(g, UNITS))
                    pe.wait_ge(down_added, s * NT + t + 1)
                    i = inter[b % 2]
                    for n in range(NCH):
                        mm = mm3(pe, bank_d[t % 2][:], (i[0][:, n, t * P:(t + 1) * P], i[1][:, n, t * P:(t + 1) * P]),
                                 (wd[gp][0][:, n, :], wd[gp][1][:, n, :]), n == 0, n == NCH - 1)
                    mm.then_inc(down_mm, 1)

                for n in range(UNITS):
                    unit(0, n)
                pe.wait_ge(item_lo, START + B * ITEMS + B * NT)
                for n in range(NCH):
                    gate_up(0, 0, 0, n)

                def emit(g, gp, b, last_group):
                    nb = (b + 1) % B
                    ng, ngp = (g, gp) if nb else (g + 1, 1 - gp)
                    more = nb or not last_group
                    if more:
                        gate_up(ng, ngp, nb, 0)
                    down(g, gp, b, 0)
                    down(g, gp, b, 1)
                    if more:
                        gate_up(ng, ngp, nb, 1)
                    down(g, gp, b, 2)
                    down(g, gp, b, 3)
                    if not last_group:
                        for k in UNITS_AT[b]:
                            unit(g + 1, ORDER.index(k))

                substeps(emit, pe)

            def weight_place(k, gp):
                pairs = (wg, wg, wu, wu, wd, wd)[k][gp]
                if k < 2 * NCH:
                    return [w[:, k % NCH].rearrange("p c n -> p (c n)") for w in pairs]
                return [w[:, k - 2 * NCH, :] for w in pairs]

            @blk.scalar
            def _(act):
                act.wait_ge(scales_loaded, 48)
                for s in (gate_s, up_s, down_s):
                    act.activation(s[:], s[:], ACT.Copy, scale=4.0).then_inc(scales_times4, 1)
                with act.Fori(0, B) as b:
                    for t in range(NT):
                        act.wait_ge(item_mm, START + B * ITEMS + b * NT + t + 1)
                        act.activation(h3T[0][:, :, bass.ds(b * S + t * P, P)],
                                       acc[t][:].rearrange("p (c n) -> p c n", c=KC), ACT.Copy).then_inc(item_hi, 1)

                def unit_sign(g, n):
                    u, r = unit_index(g, n), n % 2
                    act.wait_ge(dq_bits, u + 1)
                    act.wait_ge(dq_value, START + at_least_0(u - 1))
                    act.activation(dq_c[:, r, :], dq_f[:, r, :], ACT.Sign).then_inc(dq_sign, 1)

                def unit_hi(g, n, k, gp):
                    u, r = unit_index(g, n), n % 2
                    act.wait_ge(w_mm, START + u + 1)
                    if n == 0 and not (isinstance(g, int) and g == 0):
                        act.wait_ge(down_mm, START + (g - 1) * (B * NT))
                    act.activation(weight_place(k, gp)[0], bank_w[r][:], ACT.Copy).then_inc(w_hi_made, 1)

                def elementwise(g, b, n):
                    e = (g * B + b) * NCH + n
                    act.wait_ge(gu_mm, e * 2 + 2)
                    act.wait_ge(in_lo_made, START + at_least_0(e - 1))
                    act.activation(act_buf[n][:], bank_g[n][:], ACT.Square).then_inc(sq_made, 1)
                    act.wait_ge(z_made, e + 1)
                    act.activation(act_buf[n][:], act_buf[n][:], ACT.Tanh, scale=GELU_A * GELU_B).then_inc(tanh_made, 1)
                    act.wait_ge(v_made, START + e + 1)
                    if n == 0:
                        act.wait_ge(down_mm, START + at_least_0((g * B + b - 1) * NT))
                    act.activation(inter[b % 2][0][:, n, :], act_buf[n][:], ACT.Copy).then_inc(in_hi_made, 1)

                for n, k in enumerate(ORDER):
                    unit_sign(0, n)
                    unit_hi(0, n, k, 0)
                for n in range(NCH):
                    elementwise(0, 0, n)

                def emit(g, gp, b, last_group):
                    nb = (b + 1) % B
                    ng = g if nb else g + 1
                    more = nb or not last_group
                    units = [] if last_group else [ORDER.index(k) for k in UNITS_AT[b]]
                    for n in range(NCH):
                        if n < len(units):
                            unit_sign(g + 1, units[n])
                        if more:
                            elementwise(ng, nb, n)
                    for n in units:
                        unit_hi(g + 1, n, ORDER[n], 1 - gp)

                substeps(emit, act)

            @blk.vector
            def _(dve):
                dve.sem_inc(down_added, 2)
                with dve.Fori(0, B) as b:
                    layer_norm_stats(dve, b + 2 * B, lambda t: x[:, b * NT + t, :])
                    dve.wait_ge(item_mm, START + B * ITEMS + b * NT)
                    layer_norm_scale(dve, b + 2 * B, lambda t: x[:, b * NT + t, :])
                    for t in range(NT):
                        dve.wait_ge(item_hi, START + B * ITEMS + b * NT + t + 1)
                        dve.tensor_tensor(h3T[1][:, :, bass.ds(b * S + t * P, P)],
                                          acc[t][:].rearrange("p (c n) -> p c n", c=KC),
                                          f32(h3T[0][:, :, bass.ds(b * S + t * P, P)]), ALU.subtract)\
                           .then_inc(item_lo, 1)

                def unit_codes(g, n, k):
                    u, r = unit_index(g, n), n % 2
                    if k < 2 * NCH:
                        src = packed[:, k // NCH, (k % NCH) * 256:(k % NCH) * 256 + 256]
                        dst = dq_f[:, r, :].bitcast(I32).rearrange("p (k e) -> p k e", e=2)
                        dve.wait_ge(packed_loaded[0], g * 32 + 32)
                        parts = [(dst[:, :, e], src) for e in range(2)]
                    else:
                        j = k - 2 * NCH
                        src = packed[:, 2, :].rearrange("p (t k) -> p t k", t=KC)[:, :, j * 64:(j + 1) * 64]
                        dst = dq_f[:, r, :].bitcast(I32).rearrange("p (t k e) -> p t k e", t=KC, e=2)
                        dve.wait_ge(packed_loaded[1], g * 16 + 16)
                        parts = [(dst[:, :, :, e], src) for e in range(2)]
                    dve.wait_ge(dq_sum, START + at_least_0(u - 1))
                    for e, (d, s) in enumerate(parts):
                        dve.tensor_scalar(d, s, 28 - 4 * e, 6, ALU.logical_shift_left, ALU.arith_shift_right)\
                           .then_inc(dq_shift, 1)
                    dve.wait_ge(dq_shift, START + u * 2 + 2)
                    f = dq_f[:, r, :].bitcast(I32)
                    dve.tensor_scalar(f, f, CODE_MASK, CODE_EXP, ALU.bitwise_and, ALU.bitwise_or).then_inc(dq_bits, 1)

                def unit_clamp(g, n):
                    u, r = unit_index(g, n), n % 2
                    dve.wait_ge(dq_bits, u + 1)
                    dve.wait_ge(dq_value, START + at_least_0(u - 1))
                    dve.tensor_scalar(dq_g[:, r, :], dq_f[:, r, :], -0.25, 0.25, ALU.max, ALU.min).then_inc(dq_clamp, 1)

                def unit_value(g, n):
                    u, r = unit_index(g, n), n % 2
                    dve.wait_ge(dq_sum, START + u + 1)
                    dve.wait_ge(dq_sign, u + 1)
                    dve.wait_ge(dq_weight, START + at_least_0(u - 1))
                    dve.scalar_tensor_tensor(out=dq_c[:, r, :], in0=dq_c[:, r, :], scalar=-0.25, in1=dq_g[:, r, :],
                                             op0=ALU.mult, op1=ALU.add).then_inc(dq_value, 1)

                def unit_lo(g, n, k, gp):
                    u, r = unit_index(g, n), n % 2
                    dve.wait_ge(w_hi_made, u + 1)
                    hi, lo = weight_place(k, gp)
                    dve.tensor_tensor(lo, bank_w[r][:], f32(hi), ALU.subtract).then_inc(w_lo_made, 1)

                def elementwise_z(g, b, n):
                    e = (g * B + b) * NCH + n
                    dve.wait_ge(sq_made, e + 1)
                    dve.scalar_tensor_tensor(out=act_buf[n][:], in0=act_buf[n][:], scalar=1.0 / GELU_B,
                                             in1=bank_g[n][:], op0=ALU.add, op1=ALU.mult).then_inc(z_made, 1)

                def elementwise_v(g, b, n):
                    e = (g * B + b) * NCH + n
                    dve.wait_ge(tanh_made, e + 1)
                    dve.scalar_tensor_tensor(out=act_buf[n][:], in0=act_buf[n][:], scalar=1.0, in1=bank_g[n][:],
                                             op0=ALU.add, op1=ALU.mult).then_inc(a_made, 1)
                    dve.wait_ge(a_made, e + 1)
                    dve.scalar_tensor_tensor(out=act_buf[n][:], in0=act_buf[n][:], scalar=0.5, in1=bank_u[n][:],
                                             op0=ALU.mult, op1=ALU.mult).then_inc(v_made, 1)

                def elementwise_lo(g, b, n):
                    e = (g * B + b) * NCH + n
                    dve.wait_ge(in_hi_made, e + 1)
                    i = inter[b % 2]
                    dve.tensor_tensor(i[1][:, n, :], act_buf[n][:], f32(i[0][:, n, :]), ALU.subtract)\
                       .then_inc(in_lo_made, 1)

                def add_down(g, b, t):
                    s = g * B + b
                    dve.wait_ge(down_mm, START + s * NT + t + 1)
                    xt = x[:, b * NT + t, :]
                    dve.tensor_tensor(xt, bank_d[t % 2][:], xt, ALU.add).then_inc(down_added, 1)

                for n, k in enumerate(ORDER):
                    unit_codes(0, n, k)
                    unit_clamp(0, n)
                    unit_value(0, n)
                    unit_lo(0, n, k, 0)
                for n in range(NCH):
                    elementwise_z(0, 0, n)
                    elementwise_v(0, 0, n)
                    elementwise_lo(0, 0, n)

                def emit(g, gp, b, last_group):
                    nb = (b + 1) % B
                    ng = g if nb else g + 1
                    more = nb or not last_group
                    units = [] if last_group else [ORDER.index(k) for k in UNITS_AT[b]]
                    for n in range(NCH):
                        if n < len(units):
                            unit_codes(g + 1, units[n], ORDER[units[n]])
                        if more:
                            elementwise_z(ng, nb, n)
                        if n < len(units):
                            unit_clamp(g + 1, units[n])
                        if more:
                            elementwise_v(ng, nb, n)
                        if n < len(units):
                            unit_value(g + 1, units[n])
                        if more:
                            elementwise_lo(ng, nb, n)
                        add_down(g, b, 2 * n)
                        add_down(g, b, 2 * n + 1)
                    for n in units:
                        unit_lo(g + 1, n, ORDER[n], 1 - gp)

                substeps(emit, dve)


_INS = ['x', 'ctx_1024', 'L0_attn_Wq', 'L0_attn_bq', 'L0_attn_Wk', 'L0_attn_bk', 'L0_attn_Wv', 'L0_attn_bv',
        'L0_attn_Wo', 'L0_attn_bo', 'L0_xattn_Wq', 'L0_xattn_bq', 'L0_xattn_Wk', 'L0_xattn_bk',
        'L0_ffn_gate_W_packed', 'L0_ffn_gate_scales', 'L0_ffn_up_W_packed', 'L0_ffn_up_scales',
        'L0_ffn_down_W_packed', 'L0_ffn_down_scales']


def kernel(**inputs):
    import numpy as _np
    import concourse.bacc as _bacc
    from concourse import mybir as _mybir
    from concourse.bass_utils import run_bass_kernel_spmd as _run

    nc = _bacc.Bacc("TRN2", target_bir_lowering=False, num_devices=1)
    arrays, args = {}, []
    for name in _INS:
        a = _np.ascontiguousarray(inputs[name])
        arrays[f"in_{name}_dram"] = a
        args.append(nc.dram_tensor(f"in_{name}_dram", a.shape, _mybir.dt.from_np(a.dtype), kind="ExternalInput").ap())
    out = nc.dram_tensor("out_0_dram", inputs["x"].shape, _mybir.dt.float32, kind="ExternalOutput").ap()
    decoder_layer(nc, *args, out)
    r = _run(nc, [arrays], core_ids=[0])
    return r.results[0]["out_0_dram"]
```

```python
from contextlib import ExitStack

import numpy as np

import concourse.bass as bass
from concourse import mybir

F32 = mybir.dt.float32
F32R = mybir.dt.float32r
I32 = mybir.dt.int32
ACT = mybir.ActivationFunctionType
ALU = mybir.AluOpType
AX = mybir.AxisListType

P = 128
EPS = 1e-5


def decoder_layer(nc, x_in, ctx_in, wq_in, bq_in, wk_in, bk_in, wv_in, bv_in, wo_in, bo_in, xwq_in, xbq_in, xwk_in,
                  xbk_in, gate_in, gate_s_in, up_in, up_s_in, down_in, down_s_in, out):
    B, S, D = x_in.shape
    C = ctx_in.shape[2]
    HD = wk_in.shape[1]
    H = wq_in.shape[1] // HD
    F = gate_in.shape[0]
    NT = S // P
    KC = D // P
    CC = C // P
    SCALE = float(1.0 / np.sqrt(np.float32(HD)))
    assert HD == P and S == 512 and D == S and NT == 4 and KC == 4 and H % 2 == 0

    TILES = (H + 1) * NT
    XH = H
    LN1, CTX, KEY, VALT, XQ, XK, VAL = 0, 4, 6, 7, 8, 9, 10
    ITEMS = 11
    SPLITS = ITEMS - 1
    LAST = H + 3
    LOOP0, LOOP1 = 4, H - 2
    LNS = 2 * B

    NG = 256
    NCH = NG // P
    G = F // NG
    STEPS = G * B
    UNITS = 3 * NCH
    UNITS_AT = [[0, 2], [1, 3], [4, 5], []]
    ORDER = [u for at in UNITS_AT for u in at]
    BLK = 32
    assert G % 2 == 0 and B == 4

    def tiles_before(b, h, j=0):
        return b * TILES + h * NT + j

    ctx = ExitStack()
    with ctx:
        def sem(name):
            return ctx.enter_context(nc.semaphore(name))

        def keep(name, shape, dt=F32):
            return ctx.enter_context(nc.sbuf_tensor(name, shape, dt))

        psum = [ctx.enter_context(nc.psum_tensor(f"bank{n}", [P, 512], F32)) for n in range(8)]
        acc = psum[0:4]
        ps_s = psum[4:6]
        ps_t = psum[6]
        ps_qv = psum[7]

        x = keep("x", [P, B * NT, D])
        ident = keep("ident", [P, P])
        neg_half = keep("neg_half", [P, NT])
        stats = keep("stats", [P, NT, 6])
        mv = keep("mv", [P, NT, 2])
        ve = keep("ve", [P, NT])
        rstd = keep("rstd", [P, NT])
        hn = keep("hn", [P, NT, D])
        packed = keep("packed", [P, 3, 512], I32)
        gate_s = keep("gate_s", [P, F // P, D // BLK])
        up_s = keep("up_s", [P, F // P, D // BLK])
        down_s = keep("down_s", [P, KC, F // BLK])

        x_loaded = [sem("x_first_loaded"), sem("x_rest_loaded")]
        small_loaded = sem("small_loaded")
        ctx_loaded = sem("ctx_loaded")
        wq_loaded = [sem(f"wq_loaded{n}") for n in range(2)]
        wo_loaded = [sem(f"wo_loaded{n}") for n in range(2)]
        packed_loaded = [sem(f"packed_loaded{n}") for n in range(2)]
        scales_loaded = sem("scales_loaded")
        const_made = sem("const_made")
        once_mm = sem("once_mm")
        once_hi = sem("once_hi")
        once_lo = sem("once_lo")
        ln_bn = sem("ln_bn")
        ln_mv = sem("ln_mv")
        ln_ve = sem("ln_ve")
        ln_rstd = sem("ln_rstd")
        h_ready = sem("h_ready")
        bo_added = sem("bo_added")
        held = sem("held")
        item_mm = sem("item_mm")
        item_pre = sem("item_pre")
        item_hi = sem("item_hi")
        item_lo = sem("item_lo")
        l2_mm = sem("l2_mm")
        l2_hi = sem("l2_hi")
        l2_lo = sem("l2_lo")
        l3_mm = sem("l3_mm")
        l3_hi = sem("l3_hi")
        l3_lo = sem("l3_lo")
        wq_hi_made = sem("wq_hi_made")
        wq_lo_made = sem("wq_lo_made")
        wo_hi_made = sem("wo_hi_made")
        wo_lo_made = sem("wo_lo_made")
        q_mm = sem("q_mm")
        q_hi_made = sem("q_hi_made")
        q_lo_made = sem("q_lo_made")
        s_mm = sem("s_mm")
        max_made = sem("max_made")
        exp_made = sem("exp_made")
        rsum_inv = sem("rsum_inv")
        p_normed = sem("p_normed")
        t_mm = sem("t_mm")
        pt_hi_made = sem("pt_hi_made")
        pt_lo_made = sem("pt_lo_made")
        pv_mm = sem("pv_mm")
        at_hi_made = sem("at_hi_made")
        at_lo_made = sem("at_lo_made")
        wo_mm = sem("wo_mm")
        acc_ready = sem("acc_ready")
        att_added = sem("att_added")
        xm_mm = sem("xm_mm")
        xm_added = sem("xm_added")
        scales_times4 = sem("scales_times4")
        dq_shift = sem("dq_shift")
        dq_bits = sem("dq_bits")
        dq_sign = sem("dq_sign")
        dq_clamp = sem("dq_clamp")
        dq_sum = sem("dq_sum")
        dq_value = sem("dq_value")
        dq_weight = sem("dq_weight")
        w_mm = sem("w_mm")
        w_hi_made = sem("w_hi_made")
        w_lo_made = sem("w_lo_made")
        gu_mm = sem("gu_mm")
        sq_made = sem("sq_made")
        z_made = sem("z_made")
        tanh_made = sem("tanh_made")
        a_made = sem("a_made")
        v_made = sem("v_made")
        in_hi_made = sem("in_hi_made")
        in_lo_made = sem("in_lo_made")
        down_mm = sem("down_mm")
        down_added = sem("down_added")
        stored = sem("stored")

        def mm3(pe, bank, w, m, start, stop):
            pe.matmul(bank, w[0], m[0], start=start, stop=False, skip_group_check=True)
            pe.matmul(bank, w[0], m[1], start=False, stop=False, skip_group_check=True)
            return pe.matmul(bank, w[1], m[0], start=False, stop=stop, skip_group_check=True)

        START = 1
        pe_started = (item_mm, l2_mm, l3_mm, acc_ready, xm_mm, pv_mm, wo_mm, s_mm, t_mm, q_mm, w_mm, down_mm)
        act_started = (item_hi, l2_hi, l3_hi, wq_hi_made, wo_hi_made, q_hi_made, at_hi_made, pt_hi_made, exp_made)
        dve_started = (item_lo, l2_lo, l3_lo, item_pre, xm_added, q_lo_made, at_lo_made, pt_lo_made, max_made, p_normed, dq_shift,
                       dq_value, w_lo_made, v_made, in_lo_made, h_ready)
        pool_started = (wq_lo_made, wo_lo_made, dq_sum, dq_weight)

        def start(engine, sems):
            for s in sems:
                engine.sem_inc(s, START)

        def at_least_0(n):
            return max(n, 0) if isinstance(n, int) else n

        def hold(engine):
            engine.sem_inc(held, 1)

        def f32(ap):
            return ap.bitcast(F32)

        def layer_norm_stats(dve, n, xt):
            for t in range(NT):
                dve.bn_stats(stats[:, t, :], xt(t)).then_inc(ln_bn, 1)
            dve.wait_ge(ln_bn, n * NT + NT)
            hold(dve)
            for t in range(NT):
                dve.bn_aggr(mv[:, t, :], stats[:, t, :]).then_inc(ln_mv, 1)

        def layer_norm_scale(dve, n, xt):
            dve.wait_ge(ln_rstd, n + 1)
            for t in range(NT):
                dve.tensor_scalar(hn[:, t, :], xt(t), mv[:, t, 0:1], rstd[:, t:t + 1], ALU.subtract,
                                  ALU.mult).then_inc(h_ready, 1)

        def layer_norm_rstd(pool, n):
            pool.wait_ge(ln_mv, n * NT + NT)
            hold(pool)
            pool.tensor_scalar(ve[:], mv[:, :, 1], EPS, None, ALU.add).then_inc(ln_ve, 1)
            pool.wait_ge(ln_ve, n + 1)
            pool.tensor_tensor(rstd[:], ve[:], neg_half[:], ALU.pow).then_inc(ln_rstd, 1)

        gate_dram = gate_in.rearrange("(g n p) k -> p g n k", p=P, n=NCH)
        up_dram = up_in.rearrange("(g n p) k -> p g n k", p=P, n=NCH)
        down_dram = down_in.rearrange("(t p) (g k) -> p g t k", p=P, k=NG // 2)

        def load_codes(sp, g):
            sp.dma_start(packed[:, 0, :].rearrange("p (n k) -> p n k", n=NCH), gate_dram[:, g])\
              .then_inc(packed_loaded[0], 16)
            sp.dma_start(packed[:, 1, :].rearrange("p (n k) -> p n k", n=NCH), up_dram[:, g])\
              .then_inc(packed_loaded[0], 16)
            sp.dma_start(packed[:, 2, :].rearrange("p (t k) -> p t k", t=KC), down_dram[:, g])\
              .then_inc(packed_loaded[1], 16)

        with ExitStack() as att:
            def sb(name, shape, dt=F32):
                return att.enter_context(nc.sbuf_tensor(name, shape, dt))

            def pair(name, shape):
                return sb(name + "_hi", shape, F32R), sb(name + "_lo", shape, F32R)

            hT = pair("hT", [P, KC, S])
            kT = pair("kT", [P, S])
            v = pair("v", [P, NT, HD])
            kf = sb("kf", [P, S])
            vf = sb("vf", [P, S])
            wkv_p = pair("wkv", [P, 2, KC, HD])
            bq = sb("bq", [P, H])
            bk = sb("bk", [P, 1])
            bv = sb("bv", [P, 1])
            bo = sb("bo", [P, D])
            xbq = sb("xbq", [P, 1])
            xbk = sb("xbk", [P, 1])
            xwT = pair("xwT", [P, 2, CC, HD])
            ctx_sb = sb("ctx_sb", [P, NT, C])
            ctxT = pair("ctxT", [P, CC, S])
            xq = pair("xq", [P, S])
            xk = pair("xk", [P, S])
            zeros = sb("zeros", [P, S], F32R)
            wq_st = sb("wq_st", [P, 2, KC, HD])
            wo_st = sb("wo_st", [P, 2, D])
            wq = [pair(f"wq{n}", [P, KC, HD]) for n in range(2)]
            wo = [pair(f"wo{n}", [P, D]) for n in range(2)]
            q = [pair(f"q{n}", [P, S]) for n in range(2)]
            prob = sb("prob", [P, 2, NT, S])
            wkv = prob[:, 0, 0:2, :].rearrange("p a (c d) -> p a c d", c=KC)
            xw = prob[:, 1, 0, :].rearrange("p (a c) -> p a c", a=2)
            neg_max = sb("neg_max", [P, 2, NT])
            rsum = sb("rsum", [P, 2, NT])
            rinv = sb("rinv", [P, 2, NT])
            pT = [pair(f"pT{n}", [P, NT, S]) for n in range(2)]
            at = [pair(f"at{n}", [P, S]) for n in range(2)]
            l2T = pT[(H - 1) % 2]
            xpT = pT[XH % 2]

            wq_dram = wq_in.rearrange("(c p) (h d) -> p c h d", p=P, d=HD)
            wo_dram = wo_in.rearrange("(h d) n -> d h n", d=HD)
            ctx_dram = ctx_in.rearrange("b (t p) c -> b p t c", p=P)
            x_dram = x_in.rearrange("b (t p) n -> b p t n", p=P)
            SMALL_LOADS = 11

            def at_work(i, lag, n):
                return not isinstance(i, int) or 0 <= i - lag < n

            def last_use(b, per, h):
                return START + b * per + at_least_0(h - 1) * (per // H)

            ITEM_AT = {(H, 2): 0, (H, 3): 1, (H + 1, 2): 2, (H + 1, 3): 3, (H + 2, 0): CTX, (H + 2, 1): CTX + 1,
                       (H + 2, 2): KEY}
            ITEMS_AFTER = (VALT, XQ, XK, VAL)
            ITEM_BANK = [ps_qv] * 4 + [ps_s[0], ps_s[1], ps_qv, ps_qv, ps_s[0], ps_s[1], ps_t]

            def split_count(b, n):
                return START + b * SPLITS + (n + 1 if n < VALT else n)

            def item_at(i, j):
                return ITEM_AT.get((i, j)) if isinstance(i, int) else None

            def pipeline(engine, b, iteration, more):
                for i in range(2, LOOP0):
                    iteration(b, i, i % 2, more)
                with engine.Fori(0, (LOOP1 - LOOP0) // 2) as n:
                    for par in range(2):
                        iteration(b, n * 2 + (LOOP0 + par), par, more)
                for i in range(LOOP1, LAST + 1):
                    iteration(b, i, i % 2, more)

            def batches(engine, batch):
                with engine.Fori(0, B - 1) as b:
                    batch(b, True)
                batch(B - 1, False)

            def ln_index(b, second, more=True):
                if second:
                    return b * 2 + (2 if more else 1)
                return 0 if isinstance(b, int) and b == 0 else b * 2 - 1

            blk = att.enter_context(nc.Block())

            @blk.sync
            def _(sp):
                def load_x(b):
                    sp.dma_start(x[:, b * NT:(b + 1) * NT, :], x_dram[b]).then_inc(x_loaded[min(b, 1)], 16)

                load_x(0)
                with nc.allow_non_contiguous_dma(reason="biases as columns, once"):
                    for dst, src in (
                        (wkv[:, 0], wk_in.rearrange("(c p) d -> p c d", p=P)),
                        (wkv[:, 1], wv_in.rearrange("(c p) d -> p c d", p=P)),
                        (xw[:, 0, :], xwq_in), (xw[:, 1, :], xwk_in),
                        (bk[:], bk_in.rearrange("(p a) -> p a", a=1)),
                        (xbq[:], xbq_in.rearrange("(p a) -> p a", a=1)),
                        (xbk[:], xbk_in.rearrange("(p a) -> p a", a=1)),
                        (bv[:], bv_in.rearrange("(p a) -> p a", a=1)),
                        (bo[:], bo_in.partition_broadcast(P)),
                    ):
                        sp.dma_start(dst, src).then_inc(small_loaded, 16)
                    for n in range(2):
                        half = slice(n * H // 2, (n + 1) * H // 2)
                        sp.dma_start(bq[:, half], bq_in.rearrange("(h d) -> d h", d=HD)[:, half])\
                          .then_inc(small_loaded, 16)
                sp.dma_start(ctx_sb[:], ctx_dram[0]).then_inc(ctx_loaded, 16)

                def load_wq(b, h, p, wrap=0):
                    sp.wait_ge(wq_lo_made, last_use(b, H, h))
                    sp.dma_start(wq_st[:, p], wq_dram[:, :, h - wrap, :]).then_inc(wq_loaded[p], 16)

                def iteration(b, i, par, more):
                    if at_work(i, -2, H):
                        load_wq(b, i + 2, par)
                    elif more and i + 2 < H + 2:
                        load_wq(b, i + 2, par, H)
                    if at_work(i, 1, H):
                        p = 1 - par
                        sp.wait_ge(wo_lo_made, last_use(b, H, i - 1))
                        sp.dma_start(wo_st[:, p], wo_dram[:, i - 1, :]).then_inc(wo_loaded[p], 16)

                for i in (-2, -1):
                    iteration(0, i, i % 2, True)
                for b in range(1, B):
                    load_x(b)
                for i in (0, 1):
                    iteration(0, i, i % 2, True)

                def batch(b, more):
                    if not more:
                        with nc.allow_non_contiguous_dma(reason="scales"):
                            for dst, src in ((gate_s, gate_s_in), (up_s, up_s_in), (down_s, down_s_in)):
                                sp.dma_start(dst[:], src.rearrange("(n p) k -> p n k", p=P))\
                                  .then_inc(scales_loaded, 16)
                        load_codes(sp, 0)
                    if more:
                        sp.wait_ge(item_mm, START + b * ITEMS + CTX + 2)
                        sp.dma_start(ctx_sb[:], ctx_dram[b + 1]).then_inc(ctx_loaded, 16)
                    pipeline(sp, b, iteration, more)
                    if more:
                        for i in (0, 1):
                            iteration(b + 1, i, i % 2, True)

                batches(sp, batch)

            @blk.gpsimd
            def _(pool):
                start(pool, pool_started)
                pool.memset(ident[:], 0.0).then_inc(const_made, 1)
                pool.wait_ge(const_made, 1)
                pool.affine_select(out=ident[:], in_=ident[:], compare_op=ALU.not_equal, fill=1.0, base=0,
                                   pattern=[[-1, P]], channel_multiplier=1).then_inc(const_made, 1)
                pool.memset(neg_half[:], -0.5).then_inc(const_made, 1)
                pool.wait_ge(const_made, 3)

                def add_bo(b, t):
                    pool.wait_ge(h_ready, START + ln_index(b, False) * NT + t + 1)
                    pool.tensor_tensor(x[:, b * NT + t, :], x[:, b * NT + t, :], bo[:], ALU.add)\
                        .then_inc(bo_added, 1)

                def iteration(b, i, par, more):
                    p = 1 - par
                    if at_work(i, -1, H) or (more and i == H - 1):
                        pool.wait_ge(wq_hi_made, START + b * H + i + 2)
                        pool.tensor_tensor(wq[p][1][:], wq_st[:, p], f32(wq[p][0][:]), ALU.subtract)\
                            .then_inc(wq_lo_made, 1)
                    if at_work(i, 3, H):
                        pool.wait_ge(wo_hi_made, START + b * H + i - 2)
                        pool.tensor_tensor(wo[p][1][:], wo_st[:, p], f32(wo[p][0][:]), ALU.subtract)\
                            .then_inc(wo_lo_made, 1)
                    if more and isinstance(i, int) and i == H - 2:
                        layer_norm_rstd(pool, ln_index(b + 1, False))
                    if more and isinstance(i, int) and H <= i < H + NT:
                        add_bo(b + 1, i - H)

                layer_norm_rstd(pool, 0)
                iteration(0, -1, 1, True)
                pool.wait_ge(small_loaded, 16 * SMALL_LOADS)
                for t in range(NT):
                    add_bo(0, t)
                for i in (0, 1):
                    iteration(0, i, i % 2, True)

                def batch(b, more):
                    pipeline(pool, b, iteration, more)
                    layer_norm_rstd(pool, ln_index(b, True, more))
                    if more:
                        for i in (0, 1):
                            iteration(b + 1, i, i % 2, True)

                batches(pool, batch)

            @blk.tensor
            def _(pe):
                start(pe, pe_started)
                pe.wait_ge(const_made, 3)
                pe.wait_ge(small_loaded, 16 * SMALL_LOADS)
                for n in range(2):
                    for c in range(CC):
                        mm = pe.transpose(ps_qv[:, (n * CC + c) * P:(n * CC + c + 1) * P],
                                          xw[:, n, c * P:(c + 1) * P], ident[:])
                mm.then_inc(once_mm, 1)
                pe.wait_ge(once_lo, 3)

                def item(b, n, bank):
                    if n < CTX:
                        pe.wait_ge(h_ready, START + ln_index(b, False) * NT + n + 1)
                        for c in range(KC):
                            mm = pe.transpose(bank[:, c * P:(c + 1) * P], hn[:, n, c * P:(c + 1) * P], ident[:])
                    elif n < KEY:
                        pe.wait_ge(ctx_loaded, b * 16 + 16)
                        for m in range(2):
                            for c in range(CC):
                                mm = pe.transpose(bank[:, (m * CC + c) * P:(m * CC + c + 1) * P],
                                                  ctx_sb[:, 2 * (n - CTX) + m, c * P:(c + 1) * P], ident[:])
                    elif n == KEY:
                        pe.wait_ge(item_lo, split_count(b, LN1 + NT - 1))
                        for c in range(KC):
                            mm = mm3(pe, bank[:], (wkv_p[0][:, 0, c, :], wkv_p[1][:, 0, c, :]),
                                     (hT[0][:, c, :], hT[1][:, c, :]), c == 0, c == KC - 1)
                    elif n == VALT:
                        pe.wait_ge(item_pre, START + b * 2 + 1)
                        for c in range(KC):
                            mm = mm3(pe, bank[:], (wkv_p[0][:, 1, c, :], wkv_p[1][:, 1, c, :]),
                                     (hT[0][:, c, :], hT[1][:, c, :]), c == 0, c == KC - 1)
                    elif n == VAL:
                        pe.wait_ge(item_pre, START + b * 2 + 2)
                        pe.wait_ge(pt_lo_made, START + b * TILES)
                        for t in range(NT):
                            mm = pe.transpose(bank[:, t * P:(t + 1) * P], vf[:, t * P:(t + 1) * P], ident[:])
                    else:
                        pe.wait_ge(item_lo, split_count(b, CTX + 1))
                        for c in range(CC):
                            mm = mm3(pe, bank[:], (xwT[0][:, n - XQ, c, :], xwT[1][:, n - XQ, c, :]),
                                     (ctxT[0][:, c, :], ctxT[1][:, c, :]), c == 0, c == CC - 1)
                    mm.then_inc(item_mm, 1)

                def item_in_pipeline(b, i, n):
                    if n in (0, 2, KEY):
                        pe.wait_ge(at_lo_made, START + b * H + i - 2)
                    elif n in (1, 3):
                        pe.wait_ge(item_lo, split_count(b + 1, n - 1))
                    elif n in (CTX, CTX + 1):
                        pe.wait_ge(exp_made, START + tiles_before(b, XH, 3 + n - CTX))
                    item(b + 1, n, ITEM_BANK[n])

                def queries(b, i, par, half):
                    if half == 0:
                        pe.wait_ge(wq_lo_made, START + b * H + i + 1)
                        if isinstance(i, int) and i == 0:
                            pe.wait_ge(item_pre, START + b * 2 + 2)
                        elif isinstance(i, int) and i < 3:
                            pe.wait_ge(q_lo_made, START + b * H + i)
                        else:
                            pe.wait_ge(at_lo_made, START + b * H + i - 2)
                    for c in (2 * half, 2 * half + 1):
                        mm = mm3(pe, ps_qv[:], (wq[par][0][:, c, :], wq[par][1][:, c, :]),
                                 (hT[0][:, c, :], hT[1][:, c, :]), c == 0, c == KC - 1)
                    if half:
                        mm.then_inc(q_mm, 1)

                def cross_product(b, t):
                    if t == 0:
                        pe.wait_ge(l2_lo, START + b * NT + NT)
                    for c in range(KC):
                        mm = mm3(pe, acc[t][:], (l2T[0][:, c, t * P:(t + 1) * P], l2T[1][:, c, t * P:(t + 1) * P]),
                                 (xpT[0][:, c, :], xpT[1][:, c, :]), c == 0, c == KC - 1)
                    mm.then_inc(xm_mm, 1)

                def project(b, i, par, j):
                    h, p = i - 4, par
                    if j == 0:
                        pe.wait_ge(wo_lo_made, START + b * H + h + 1)
                        pe.wait_ge(at_lo_made, START + b * H + h + 1)
                    last = isinstance(i, int) and h == H - 1
                    mm = mm3(pe, acc[j][:], (at[p][0][:, j * P:(j + 1) * P], at[p][1][:, j * P:(j + 1) * P]),
                             (wo[p][0][:], wo[p][1][:]), False, last)
                    if last:
                        mm.then_inc(acc_ready, 1)
                    elif j == NT - 1:
                        mm.then_inc(wo_mm, 1)

                def iteration(b, i, par, more):
                    for j in range(NT):
                        if at_work(i, 2, H + 1):
                            h, p = i - 2, par
                            pe.wait_ge(p_normed, START + tiles_before(b, h, j + 1))
                            pe.wait_ge(pt_lo_made, START + tiles_before(b, h, j))
                            for c in range(NT):
                                mm = pe.transpose(ps_t[:, c * P:(c + 1) * P], prob[:, p, j, c * P:(c + 1) * P],
                                                  ident[:])
                            mm.then_inc(t_mm, 1)
                        if j == 0 and at_work(i, 4, H):
                            project(b, i, par, 0)
                        if j < 2 and at_work(i, 3, H):
                            h, p = i - 3, 1 - par
                            if j == 0:
                                pe.wait_ge(pt_lo_made, START + tiles_before(b, h, NT))
                                if isinstance(i, int) and i > H:
                                    if more:
                                        pe.wait_ge(item_lo, split_count(b + 1, 2 * (i - H) - 1))
                                    else:
                                        pe.wait_ge(at_lo_made, START + b * H + h)
                                else:
                                    pe.wait_ge(q_lo_made, START + b * H + i)
                            for c in (2 * j, 2 * j + 1):
                                mm = mm3(pe, ps_qv[:], (v[0][:, c, :], v[1][:, c, :]),
                                         (pT[p][0][:, c, :], pT[p][1][:, c, :]), c == 0, c == NT - 1)
                            if j:
                                mm.then_inc(pv_mm, 1)
                        if j >= 2 and at_work(i, 0, H):
                            queries(b, i, par, j - 2)
                        if more and item_at(i, j) is not None:
                            item_in_pipeline(b, i, item_at(i, j))
                        if at_work(i, 1, H + 1):
                            scores(b, i - 1, 1 - par, j)
                        if j > 0 and at_work(i, 4, H):
                            project(b, i, par, j)
                    if isinstance(i, int) and i == LOOP0 - 1:
                        pe.wait_ge(xm_added, START + b * NT)
                        for t in range(NT):
                            pe.matmul(acc[t][:], zeros[:, 0:P], zeros[:], start=True, stop=False,
                                      skip_group_check=True)

                def scores(b, h, p, j):
                    cross = isinstance(h, int) and h == XH
                    if j == 0 and not cross:
                        pe.wait_ge(q_lo_made, START + b * H + h + 1)
                    if isinstance(h, int) and h == 0:
                        pe.wait_ge(item_lo, split_count(b, VAL))
                    if j > 1 or not (isinstance(h, int) and h == 0):
                        pe.wait_ge(exp_made, START - 1 + tiles_before(b, h, j))
                    qq, kk = (xq, xk) if cross else (q[p], kT)
                    mm3(pe, ps_s[j % 2][:], (qq[0][:, j * P:(j + 1) * P], qq[1][:, j * P:(j + 1) * P]),
                        (kk[0][:], kk[1][:]), True, True).then_inc(s_mm, 1)

                def second_layernorm(b, more):
                    for t in range(NT):
                        pe.wait_ge(h_ready, START + ln_index(b, True, more) * NT + t + 1)
                        for c in range(KC):
                            mm = pe.transpose(acc[t][:, c * P:(c + 1) * P], hn[:, t, c * P:(c + 1) * P], ident[:])
                        mm.then_inc(l2_mm, 1)

                def first_heads(b, before):
                    for half in range(2):
                        queries(b, 0, 0, half)
                    if before:
                        second_layernorm(b - 1, True)
                        cross_product(b - 1, 0)
                        cross_product(b - 1, 1)
                    for j in range(NT):
                        if j >= 2:
                            queries(b, 1, 1, j - 2)
                        scores(b, 0, 0, j)
                        if before and j < 2:
                            cross_product(b - 1, 2 + j)

                for n in range(ITEMS):
                    item(0, n, acc[n] if n < CTX else ITEM_BANK[n])
                first_heads(0, False)

                def batch(b, more):
                    pipeline(pe, b, iteration, more)
                    if more:
                        for n in ITEMS_AFTER:
                            item(b + 1, n, ITEM_BANK[n])
                        first_heads(b + 1, True)
                    else:
                        second_layernorm(b, more)
                        for t in range(NT):
                            cross_product(b, t)

                batches(pe, batch)

            @blk.scalar
            def _(act):
                start(act, act_started)
                act.wait_ge(small_loaded, 16 * SMALL_LOADS)
                act.activation(wkv_p[0][:], wkv, ACT.Copy).then_inc(once_hi, 1)
                act.wait_ge(once_mm, 1)
                act.activation(xwT[0][:].rearrange("p a c d -> p (a c d)"), ps_qv[:], ACT.Copy).then_inc(once_hi, 1)

                def item_hi_part(b, n, bank):
                    if n == VALT:
                        return
                    if n == KEY:
                        act.wait_ge(item_pre, START + b * 2 + 1)
                        act.activation(kT[0][:], kf[:], ACT.Copy).then_inc(item_hi, 1)
                        return
                    act.wait_ge(item_mm, START + b * ITEMS + n + 1)
                    if n < CTX:
                        act.activation(hT[0][:, :, n * P:(n + 1) * P], bank[:].rearrange("p (c n) -> p c n", c=KC),
                                       ACT.Copy).then_inc(item_hi, 1)
                    elif n < KEY:
                        m = n - CTX
                        act.activation(ctxT[0][:, :, 2 * m * P:(2 * m + 2) * P].rearrange("p c (m n) -> p m c n", m=2),
                                       bank[:].rearrange("p (m c n) -> p m c n", m=2, c=CC), ACT.Copy)\
                           .then_inc(item_hi, 1)
                    elif n == VAL:
                        act.activation(v[0][:].rearrange("p t d -> p (t d)"), bank[:], ACT.Copy).then_inc(item_hi, 1)
                    else:
                        dst, bias = ((xq, xbq), (xk, xbk))[n - XQ]
                        act.activation(dst[0][:], bank[:], ACT.Identity, bias=bias[:]).then_inc(item_hi, 1)

                def query_hi(b, i, par):
                    act.wait_ge(q_mm, START + b * H + i + 1)
                    act.wait_ge(s_mm, START + b * TILES + at_least_0(i - 1) * NT)
                    act.activation(q[par][0][:], ps_qv[:], ACT.Identity, bias=bq[:, bass.ds(i, 1)])\
                       .then_inc(q_hi_made, 1)

                def exponentials(b, h, p, j):
                    act.wait_ge(max_made, START + tiles_before(b, h, j + 1))
                    act.wait_ge(t_mm, START + b * TILES + (0 if isinstance(h, int) and h < 2
                                                           else (h - 2) * NT + j + 1))
                    act.activation(prob[:, p, j, :], ps_s[j % 2][:], ACT.Exp, bias=neg_max[:, p, j:j + 1],
                                   accum_out=rsum[:, p, j:j + 1]).then_inc(exp_made, 1)

                def wait_loaded(loaded, b, h, p):
                    act.wait_ge(loaded, b * (8 * H) + h * 8 + (16 - 8 * p))

                def query_weights_hi(b, h, p):
                    wait_loaded(wq_loaded[p], b, h, p)
                    act.wait_ge(q_mm, last_use(b, H, h))
                    act.activation(wq[p][0][:], wq_st[:, p], ACT.Copy).then_inc(wq_hi_made, 1)

                def iteration(b, i, par, more):
                    for j in range(NT):
                        if at_work(i, 2, H + 1):
                            h, p = i - 2, par
                            act.wait_ge(t_mm, START + tiles_before(b, h, j + 1))
                            if j == 0:
                                act.wait_ge(pv_mm, last_use(b, H, h))
                                if isinstance(h, int) and h < 2:
                                    act.wait_ge(xm_mm, START + b * NT)
                            act.activation(pT[p][0][:, :, j * P:(j + 1) * P],
                                           ps_t[:].rearrange("p (c n) -> p c n", c=NT), ACT.Copy)\
                               .then_inc(pt_hi_made, 1)
                        if j == 0 and at_work(i, 2, H + 1):
                            exponentials(b, i - 2, par, NT - 1)
                        if j > 0 and at_work(i, 1, H + 1):
                            exponentials(b, i - 1, 1 - par, j - 1)
                        if j == 1 and at_work(i, 3, H):
                            h, p = i - 3, 1 - par
                            act.wait_ge(pv_mm, START + b * H + h + 1)
                            act.wait_ge(wo_mm, START + b * (H - 1) + at_least_0(h - 1))
                            if isinstance(h, int) and h < 2:
                                act.wait_ge(acc_ready, START + b * NT)
                            act.activation(at[p][0][:], ps_qv[:], ACT.Copy).then_inc(at_hi_made, 1)
                        if j == NT - 1 and at_work(i, 0, H):
                            query_hi(b, i, par)
                        if more and item_at(i, j) is not None:
                            item_hi_part(b + 1, item_at(i, j), ITEM_BANK[item_at(i, j)])
                        if j == 0 and (at_work(i, -1, H) or (more and i == H - 1)):
                            query_weights_hi(b, i + 1, 1 - par)
                        if j == 2 and at_work(i, 3, H):
                            h, p = i - 3, 1 - par
                            wait_loaded(wo_loaded[p], b, h, p)
                            act.wait_ge(wo_mm, START + b * (H - 1) + at_least_0(h - 1))
                            if isinstance(h, int) and h < 2:
                                act.wait_ge(acc_ready, START + b * NT)
                            act.activation(wo[p][0][:], wo_st[:, p], ACT.Copy).then_inc(wo_hi_made, 1)

                def second_layernorm_hi(b):
                    act.wait_ge(pv_mm, START + b * H + H)
                    for t in range(NT):
                        act.wait_ge(l2_mm, START + b * NT + t + 1)
                        act.activation(l2T[0][:, :, t * P:(t + 1) * P], acc[t][:].rearrange("p (c n) -> p c n", c=KC),
                                       ACT.Copy).then_inc(l2_hi, 1)

                def first_heads(b, before):
                    query_hi(b, 0, 0)
                    query_weights_hi(b, 1, 1)
                    if before:
                        second_layernorm_hi(b - 1)
                    for j in range(NT):
                        if j > 0:
                            exponentials(b, 0, 0, j - 1)
                        if j == NT - 1:
                            query_hi(b, 1, 1)
                        if j == 0:
                            query_weights_hi(b, 2, 0)

                query_weights_hi(0, 0, 0)
                for n in range(ITEMS):
                    item_hi_part(0, n, acc[n] if n < CTX else ITEM_BANK[n])
                first_heads(0, False)

                def batch(b, more):
                    pipeline(act, b, iteration, more)
                    if more:
                        for n in ITEMS_AFTER:
                            item_hi_part(b + 1, n, ITEM_BANK[n])
                        first_heads(b + 1, True)
                    else:
                        act.wait_ge(scales_loaded, 48)
                        for s in (gate_s, up_s, down_s):
                            act.activation(s[:], s[:], ACT.Copy, scale=4.0).then_inc(scales_times4, 1)
                        second_layernorm_hi(b)

                batches(act, batch)

            @blk.vector
            def _(dve):
                start(dve, dve_started)
                dve.memset(f32(zeros[:]), 0.0).then_inc(once_lo, 1)

                def x_tile(b):
                    return lambda t: x[:, b * NT + t, :]

                def item_pre_part(b, n, bank):
                    dve.wait_ge(item_mm, START + b * ITEMS + n + 1)
                    if n == KEY:
                        dve.tensor_scalar(kf[:], bank[:], bk[:], SCALE, ALU.add, ALU.mult).then_inc(item_pre, 1)
                    else:
                        dve.tensor_scalar(vf[:], bank[:], bv[:], None, ALU.add).then_inc(item_pre, 1)

                def item_lo_part(b, n, bank, pre=True):
                    if pre and n in (KEY, VALT):
                        item_pre_part(b, n, bank)
                    if n == VALT:
                        return
                    dve.wait_ge(item_hi, split_count(b, n))
                    if n < CTX:
                        cols = slice(n * P, (n + 1) * P)
                        ins = dve.tensor_tensor(hT[1][:, :, cols], bank[:].rearrange("p (c n) -> p c n", c=KC),
                                                f32(hT[0][:, :, cols]), ALU.subtract)
                    elif n < KEY:
                        for m in range(2):
                            cols = slice((2 * (n - CTX) + m) * P, (2 * (n - CTX) + m + 1) * P)
                            ins = dve.tensor_tensor(
                                ctxT[1][:, :, cols],
                                bank[:, m * CC * P:(m + 1) * CC * P].rearrange("p (c n) -> p c n", c=CC),
                                f32(ctxT[0][:, :, cols]), ALU.subtract)
                    elif n == KEY:
                        ins = dve.tensor_tensor(kT[1][:], kf[:], f32(kT[0][:]), ALU.subtract)
                    elif n == VAL:
                        ins = dve.tensor_tensor(v[1][:].rearrange("p t d -> p (t d)"), bank[:],
                                                f32(v[0][:]).rearrange("p t d -> p (t d)"), ALU.subtract)
                    else:
                        dst, bias = ((xq, xbq), (xk, xbk))[n - XQ]
                        ins = dve.scalar_tensor_tensor(out=dst[1][:], in0=bank[:], scalar=bias[:], in1=f32(dst[0][:]),
                                                       op0=ALU.add, op1=ALU.subtract)
                    ins.then_inc(item_lo, 1)

                def normalise(b, h, p, j):
                    dve.wait_ge(exp_made, START + tiles_before(b, h, j + 1))
                    dve.reciprocal(rinv[:, p, j:j + 1], rsum[:, p, j:j + 1]).then_inc(rsum_inv, 1)
                    dve.wait_ge(rsum_inv, tiles_before(b, h, j + 1))
                    dve.tensor_scalar(prob[:, p, j, :], prob[:, p, j, :], rinv[:, p, j:j + 1], None, ALU.mult)\
                       .then_inc(p_normed, 1)

                def minus_max(b, h, p, j):
                    dve.wait_ge(s_mm, START + tiles_before(b, h, j + 1))
                    dve.tensor_reduce(neg_max[:, p, j:j + 1], ps_s[j % 2][:], AX.X, ALU.max, negate=True)\
                       .then_inc(max_made, 1)

                def query_lo(b, i, par):
                    dve.wait_ge(q_hi_made, START + b * H + i + 1)
                    dve.scalar_tensor_tensor(out=q[par][1][:], in0=ps_qv[:], scalar=bq[:, bass.ds(i, 1)],
                                             in1=f32(q[par][0][:]), op0=ALU.add, op1=ALU.subtract)\
                       .then_inc(q_lo_made, 1)

                def iteration(b, i, par, more):
                    for j in range(NT):
                        if at_work(i, 2, H + 1):
                            h, p = i - 2, par
                            dve.wait_ge(pt_hi_made, START + tiles_before(b, h, j + 1))
                            dve.tensor_tensor(pT[p][1][:, :, j * P:(j + 1) * P],
                                              ps_t[:].rearrange("p (c n) -> p c n", c=NT),
                                              f32(pT[p][0][:, :, j * P:(j + 1) * P]), ALU.subtract)\
                               .then_inc(pt_lo_made, 1)
                        if j == 0 and at_work(i, 2, H + 1):
                            normalise(b, i - 2, par, NT - 1)
                        if j > 0 and at_work(i, 1, H + 1):
                            normalise(b, i - 1, 1 - par, j - 1)
                        if j == 1 and at_work(i, 3, H):
                            h, p = i - 3, 1 - par
                            dve.wait_ge(at_hi_made, START + b * H + h + 1)
                            dve.tensor_tensor(at[p][1][:], ps_qv[:], f32(at[p][0][:]), ALU.subtract)\
                               .then_inc(at_lo_made, 1)
                        if j == NT - 1 and at_work(i, 0, H):
                            query_lo(b, i, par)
                        if more and item_at(i, j) is not None:
                            item_lo_part(b + 1, item_at(i, j), ITEM_BANK[item_at(i, j)])
                        if at_work(i, 1, H + 1):
                            minus_max(b, i - 1, 1 - par, j)
                    if more and isinstance(i, int) and i == H - 2:
                        layer_norm_stats(dve, ln_index(b + 1, False), x_tile(b + 1))
                    if more and isinstance(i, int) and i == H - 1:
                        dve.wait_ge(l2_mm, START + b * NT)
                        layer_norm_scale(dve, ln_index(b + 1, False), x_tile(b + 1))

                def add_cross(b, t):
                    dve.wait_ge(xm_mm, START + b * NT + t + 1)
                    dve.tensor_tensor(x[:, b * NT + t, :], acc[t][:], x[:, b * NT + t, :], ALU.add)\
                       .then_inc(xm_added, 1)

                def second_layernorm_lo(b):
                    for t in range(NT):
                        dve.wait_ge(l2_hi, START + b * NT + t + 1)
                        dve.tensor_tensor(l2T[1][:, :, t * P:(t + 1) * P],
                                          acc[t][:].rearrange("p (c n) -> p c n", c=KC),
                                          f32(l2T[0][:, :, t * P:(t + 1) * P]), ALU.subtract).then_inc(l2_lo, 1)

                def first_heads(b, before):
                    query_lo(b, 0, 0)
                    if before:
                        second_layernorm_lo(b - 1)
                        add_cross(b - 1, 0)
                        add_cross(b - 1, 1)
                    for j in range(NT):
                        if j > 0:
                            normalise(b, 0, 0, j - 1)
                        if j == NT - 1:
                            query_lo(b, 1, 1)
                        minus_max(b, 0, 0, j)
                        if before and j < 2:
                            add_cross(b - 1, 2 + j)

                dve.wait_ge(x_loaded[0], 16)
                layer_norm_stats(dve, 0, x_tile(0))
                dve.wait_ge(once_hi, 1)
                dve.tensor_tensor(wkv_p[1][:], wkv, f32(wkv_p[0][:]), ALU.subtract).then_inc(once_lo, 1)
                layer_norm_scale(dve, 0, x_tile(0))
                dve.wait_ge(once_hi, 2)
                dve.tensor_tensor(xwT[1][:].rearrange("p a c d -> p (a c d)"), ps_qv[:],
                                  f32(xwT[0][:].rearrange("p a c d -> p (a c d)")), ALU.subtract).then_inc(once_lo, 1)
                for n in range(ITEMS):
                    item_lo_part(0, n, acc[n] if n < CTX else ITEM_BANK[n])
                dve.wait_ge(x_loaded[1], 16 * (B - 1))
                first_heads(0, False)

                def batch(b, more):
                    pipeline(dve, b, iteration, more)
                    dve.wait_ge(bo_added, b * NT + NT)
                    for t in range(NT):
                        dve.wait_ge(acc_ready, START + b * NT + t + 1)
                        dve.tensor_tensor(x[:, b * NT + t, :], acc[t][:], x[:, b * NT + t, :], ALU.add)\
                           .then_inc(att_added, 1)
                    if more:
                        dve.wait_ge(item_mm, START + (b + 1) * ITEMS + LN1 + NT)
                    dve.wait_ge(att_added, b * NT + NT)
                    hold(dve)
                    layer_norm_stats(dve, ln_index(b, True, more), x_tile(b))
                    if more:
                        item_pre_part(b + 1, VALT, ITEM_BANK[VALT])
                    layer_norm_scale(dve, ln_index(b, True, more), x_tile(b))
                    if more:
                        for n in ITEMS_AFTER:
                            item_lo_part(b + 1, n, ITEM_BANK[n], pre=False)
                        first_heads(b + 1, True)
                    else:
                        second_layernorm_lo(b)
                        for t in range(NT):
                            add_cross(b, t)

                batches(dve, batch)

        with ExitStack() as ffn:
            def sb(name, shape, dt=F32):
                return ffn.enter_context(nc.sbuf_tensor(name, shape, dt))

            def pair(name, shape):
                return sb(name + "_hi", shape, F32R), sb(name + "_lo", shape, F32R)

            h3T = pair("h3T", [P, KC, B * S])
            wg = [pair(f"wg{n}", [P, NCH, KC, P]) for n in range(2)]
            wu = [pair(f"wu{n}", [P, NCH, KC, P]) for n in range(2)]
            wd = [pair(f"wd{n}", [P, NCH, D]) for n in range(2)]
            inter = [pair(f"inter{n}", [P, NCH, S]) for n in range(2)]
            act_buf = [sb(f"act_buf{n}", [P, S]) for n in range(NCH)]
            dq_f = sb("dq_f", [P, 2, 512])
            dq_g = sb("dq_g", [P, 2, 512])
            dq_c = sb("dq_c", [P, 2, 512])
            dq_w = sb("dq_w", [P, 2, 512])

            bank_g, bank_u = psum[0:2], psum[2:4]
            bank_d = psum[4:6]
            bank_w = psum[6:8]

            CODE_MASK = np.int32(np.uint32(0x81C00000).view(np.int32)).item()
            CODE_EXP = 0x3E000000
            out_dram = out.rearrange("b (t p) n -> b p t n", p=P)
            GELU_A, GELU_B = 0.7978845608028654, 0.044715

            blk = ffn.enter_context(nc.Block())

            def unit_index(g, n):
                return g * UNITS + n

            @blk.sync
            def _(sp):
                with sp.Fori(1, G) as g:
                    sp.wait_ge(dq_shift, START + g * (2 * UNITS))
                    load_codes(sp, g)
                for b in range(B):
                    sp.wait_ge(down_added, 2 + (G - 1) * B * NT + (b + 1) * NT)
                    sp.dma_start(out_dram[b], x[:, b * NT:(b + 1) * NT, :]).then_inc(stored, 16)
                sp.wait_ge(stored, 16 * B)

            def units_at(b, last_group):
                made = [[] if last_group else [ORDER.index(k) for k in at] for at in UNITS_AT]
                return (made[b][0] if made[b] else None), (made[b - 1][1] if b and made[b - 1] else None)

            def units_before(b):
                return sum(u is not None for k in range(b) for u in units_at(k, False)) + \
                    (units_at(b, False)[1] is not None)

            def substeps(emit, engine):
                for b in range(B):
                    emit(0, 0, b, True, False)
                with engine.Fori(0, G // 2 - 1) as n:
                    for k in range(2 * B):
                        emit(n * 2 + (1 + k // B), 1 - k // B, k % B, False, False)
                for b in range(B):
                    emit(G - 1, 1, b, False, True)

            AHEAD = 2
            l3_bank = (bank_g[1], bank_u[1], bank_d[0], bank_d[1])

            @blk.gpsimd
            def _(pool):
                def unit(g, n, k):
                    u, r = unit_index(g, n), n % 2
                    pool.wait_ge(dq_clamp, u + 1)
                    pool.tensor_tensor(dq_g[:, r, :], dq_g[:, r, :], dq_f[:, r, :], ALU.add).then_inc(dq_sum, 1)
                    pool.wait_ge(dq_value, START + u + 1)
                    pool.wait_ge(w_mm, START + at_least_0(u - 1))
                    if k < 2 * NCH:
                        sc = (gate_s, up_s)[k // NCH][:, bass.ds(g * NCH + k % NCH, 1), :]\
                            .rearrange("p a k -> p (a k)").unsqueeze(2).to_broadcast([P, D // BLK, BLK])
                        ins = pool.tensor_tensor(dq_w[:, r, :].rearrange("p (k e) -> p k e", e=BLK),
                                                 dq_c[:, r, :].rearrange("p (k e) -> p k e", e=BLK), sc, ALU.mult)
                    else:
                        j = k - 2 * NCH
                        sc = down_s[:, :, bass.ds(g * (NG // BLK) + j * (P // BLK), P // BLK)]\
                            .unsqueeze(3).to_broadcast([P, KC, P // BLK, BLK])
                        ins = pool.tensor_tensor(
                            dq_w[:, r, :].rearrange("p (t k e) -> p t k e", t=KC, e=BLK),
                            dq_c[:, r, :].rearrange("p (t k e) -> p t k e", t=KC, e=BLK), sc, ALU.mult)
                    ins.then_inc(dq_weight, 1)

                layer_norm_rstd(pool, LNS)
                pool.wait_ge(scales_times4, 3)
                for n, k in enumerate(ORDER):
                    if n == 2:
                        layer_norm_rstd(pool, LNS + 1)
                    unit(0, n, k)

                def emit(g, gp, b, first_group, last_group):
                    if first_group and b + AHEAD < B:
                        layer_norm_rstd(pool, LNS + b + AHEAD)
                    if not last_group:
                        for k in UNITS_AT[b]:
                            unit(g + 1, ORDER.index(k), k)

                substeps(emit, pool)

            @blk.tensor
            def _(pe):
                def l3_tile(b, t, bank):
                    pe.wait_ge(h_ready, START + (b + LNS) * NT + t + 1)
                    if b < AHEAD:
                        pe.wait_ge(l3_lo, START + b * NT)
                    else:
                        pe.wait_ge(l3_lo, START + b * NT + at_least_0(t - 1))
                        pe.wait_ge(w_lo_made, START + UNITS + units_before(b - AHEAD))
                    for c in range(KC):
                        mm = pe.transpose(bank[:, c * P:(c + 1) * P], hn[:, t, c * P:(c + 1) * P], ident[:])
                    mm.then_inc(l3_mm, 1)

                def unit(g, n, after_l3=0):
                    u, r = unit_index(g, n), n % 2
                    pe.wait_ge(dq_weight, START + u + 1)
                    pe.wait_ge(w_lo_made, START + at_least_0(u - 1))
                    if after_l3:
                        pe.wait_ge(l3_lo, START + after_l3)
                    for c in range(KC):
                        mm = pe.transpose(bank_w[r][:, c * P:(c + 1) * P], dq_w[:, r, c * P:(c + 1) * P], ident[:])
                    mm.then_inc(w_mm, 1)

                def gate_up(g, gp, b, n):
                    s = g * B + b
                    if b == 0:
                        pe.wait_ge(w_lo_made, START + unit_index(g, 2 * (n + 1)))
                    if isinstance(g, int) and g == 0:
                        pe.wait_ge(l3_lo, START + (b + 1 + (n if b == 0 else 0)) * NT)
                    pe.wait_ge(v_made, START + at_least_0((s - 1) * NCH + n + 1))
                    for w, bank in ((wg[gp], bank_g[n]), (wu[gp], bank_u[n])):
                        for c in range(KC):
                            mm = mm3(pe, bank[:], (w[0][:, n, c, :], w[1][:, n, c, :]),
                                     (h3T[0][:, c, b * S:(b + 1) * S], h3T[1][:, c, b * S:(b + 1) * S]),
                                     c == 0, c == KC - 1)
                        mm.then_inc(gu_mm, 1)

                def down(g, gp, b, t):
                    s = g * B + b
                    if t == 0:
                        pe.wait_ge(in_lo_made, START + s * NCH + NCH)
                        if b == 0:
                            pe.wait_ge(w_lo_made, START + unit_index(g, UNITS))
                    pe.wait_ge(down_added, s * NT + t + 1)
                    i = inter[b % 2]
                    for n in range(NCH):
                        mm = mm3(pe, bank_d[t % 2][:], (i[0][:, n, t * P:(t + 1) * P], i[1][:, n, t * P:(t + 1) * P]),
                                 (wd[gp][0][:, n, :], wd[gp][1][:, n, :]), n == 0, n == NCH - 1)
                    mm.then_inc(down_mm, 1)

                for t in range(NT):
                    l3_tile(0, t, l3_bank[t])
                for n in range(NCH):
                    unit(0, 2 * n)
                    unit(0, 2 * n + 1)
                    gate_up(0, 0, 0, n)
                    if n == 0:
                        for t in range(NT):
                            l3_tile(1, t, l3_bank[t])
                for n in range(2 * NCH, UNITS):
                    unit(0, n)

                def emit(g, gp, b, first_group, last_group):
                    nb = (b + 1) % B
                    ng, ngp = (g, gp) if nb else (g + 1, 1 - gp)
                    more = nb or not last_group
                    first, second = units_at(b, last_group)
                    if more:
                        gate_up(ng, ngp, nb, 0)
                    if second is not None:
                        unit(g + 1, second)
                    ln = first_group and b + AHEAD < B
                    for t in range(2):
                        if ln:
                            l3_tile(b + AHEAD, t, bank_w[t])
                    down(g, gp, b, 0)
                    down(g, gp, b, 1)
                    for t in range(2, NT):
                        if ln:
                            l3_tile(b + AHEAD, t, bank_w[t % 2])
                    if more:
                        gate_up(ng, ngp, nb, 1)
                    if first is not None:
                        unit(g + 1, first, (b + AHEAD + 1) * NT if ln else 0)
                    down(g, gp, b, 2)
                    down(g, gp, b, 3)

                substeps(emit, pe)

            def weight_place(k, gp):
                pairs = (wg, wg, wu, wu, wd, wd)[k][gp]
                if k < 2 * NCH:
                    return [w[:, k % NCH].rearrange("p c n -> p (c n)") for w in pairs]
                return [w[:, k - 2 * NCH, :] for w in pairs]

            @blk.scalar
            def _(act):
                def l3_hi_tile(b, t, bank):
                    act.wait_ge(l3_mm, START + b * NT + t + 1)
                    act.activation(h3T[0][:, :, b * S + t * P:b * S + (t + 1) * P],
                                   bank[:].rearrange("p (c n) -> p c n", c=KC), ACT.Copy).then_inc(l3_hi, 1)

                def unit_sign(g, n):
                    u, r = unit_index(g, n), n % 2
                    act.wait_ge(dq_bits, u + 1)
                    act.wait_ge(dq_value, START + at_least_0(u - 1))
                    act.activation(dq_c[:, r, :], dq_f[:, r, :], ACT.Sign).then_inc(dq_sign, 1)

                def unit_hi(g, n, k, gp):
                    u, r = unit_index(g, n), n % 2
                    act.wait_ge(w_mm, START + u + 1)
                    if n == 0 and not (isinstance(g, int) and g == 0):
                        act.wait_ge(down_mm, START + (g - 1) * (B * NT))
                    act.activation(weight_place(k, gp)[0], bank_w[r][:], ACT.Copy).then_inc(w_hi_made, 1)

                def elementwise_sq(g, b, n):
                    e = (g * B + b) * NCH + n
                    act.wait_ge(gu_mm, e * 2 + 2)
                    act.wait_ge(in_lo_made, START + at_least_0(e - 1))
                    act.activation(act_buf[n][:], bank_g[n][:], ACT.Square).then_inc(sq_made, 1)

                def elementwise_tanh(g, b, n):
                    e = (g * B + b) * NCH + n
                    act.wait_ge(z_made, e + 1)
                    act.activation(act_buf[n][:], act_buf[n][:], ACT.Tanh, scale=GELU_A * GELU_B).then_inc(tanh_made, 1)
                    act.wait_ge(v_made, START + e + 1)
                    if n == 0:
                        act.wait_ge(down_mm, START + at_least_0((g * B + b - 1) * NT))
                    act.activation(inter[b % 2][0][:, n, :], act_buf[n][:], ACT.Copy).then_inc(in_hi_made, 1)

                unit_sign(0, 0)
                for t in range(NT):
                    if t == 2:
                        unit_sign(0, 1)
                    l3_hi_tile(0, t, l3_bank[t])
                for n in range(NCH):
                    unit_hi(0, 2 * n, ORDER[2 * n], 0)
                    unit_sign(0, 2 * n + 2)
                    unit_hi(0, 2 * n + 1, ORDER[2 * n + 1], 0)
                    unit_sign(0, 2 * n + 3)
                    elementwise_sq(0, 0, n)
                    if n == 0:
                        for t in range(NT):
                            l3_hi_tile(1, t, l3_bank[t])
                    elementwise_tanh(0, 0, n)
                for n in range(2 * NCH, UNITS):
                    unit_hi(0, n, ORDER[n], 0)

                def emit(g, gp, b, first_group, last_group):
                    nb = (b + 1) % B
                    ng = g if nb else g + 1
                    more = nb or not last_group
                    units = [] if last_group else [ORDER.index(k) for k in UNITS_AT[b]]
                    first, second = units_at(b, last_group)
                    for n, transposed in enumerate((second, first)):
                        if n < len(units):
                            unit_sign(g + 1, units[n])
                        if more:
                            elementwise_sq(ng, nb, n)
                        if transposed is not None:
                            unit_hi(g + 1, transposed, ORDER[transposed], 1 - gp)
                        ln = first_group and b + AHEAD < B and n == 0
                        for t in range(2):
                            if ln:
                                l3_hi_tile(b + AHEAD, t, bank_w[t])
                        if more:
                            elementwise_tanh(ng, nb, n)
                        for t in range(2, NT):
                            if ln:
                                l3_hi_tile(b + AHEAD, t, bank_w[t % 2])

                substeps(emit, act)

            @blk.vector
            def _(dve):
                dve.sem_inc(down_added, 2)
                def l3_stats(b):
                    layer_norm_stats(dve, b + LNS, lambda t: x[:, b * NT + t, :])

                def l3_scale(b):
                    dve.wait_ge(l3_mm, START + b * NT)
                    layer_norm_scale(dve, b + LNS, lambda t: x[:, b * NT + t, :])

                def l3_lo_tile(b, t, bank):
                    dve.wait_ge(l3_hi, START + b * NT + t + 1)
                    cols = slice(b * S + t * P, b * S + (t + 1) * P)
                    dve.tensor_tensor(h3T[1][:, :, cols], bank[:].rearrange("p (c n) -> p c n", c=KC),
                                      f32(h3T[0][:, :, cols]), ALU.subtract).then_inc(l3_lo, 1)

                def unit_codes(g, n, k):
                    u, r = unit_index(g, n), n % 2
                    if k < 2 * NCH:
                        src = packed[:, k // NCH, (k % NCH) * 256:(k % NCH) * 256 + 256]
                        dst = dq_f[:, r, :].bitcast(I32).rearrange("p (k e) -> p k e", e=2)
                        dve.wait_ge(packed_loaded[0], g * 32 + 32)
                        parts = [(dst[:, :, e], src) for e in range(2)]
                    else:
                        j = k - 2 * NCH
                        src = packed[:, 2, :].rearrange("p (t k) -> p t k", t=KC)[:, :, j * 64:(j + 1) * 64]
                        dst = dq_f[:, r, :].bitcast(I32).rearrange("p (t k e) -> p t k e", t=KC, e=2)
                        dve.wait_ge(packed_loaded[1], g * 16 + 16)
                        parts = [(dst[:, :, :, e], src) for e in range(2)]
                    dve.wait_ge(dq_sum, START + at_least_0(u - 1))
                    for e, (d, s) in enumerate(parts):
                        dve.tensor_scalar(d, s, 28 - 4 * e, 6, ALU.logical_shift_left, ALU.arith_shift_right)\
                           .then_inc(dq_shift, 1)
                    dve.wait_ge(dq_shift, START + u * 2 + 2)
                    f = dq_f[:, r, :].bitcast(I32)
                    dve.tensor_scalar(f, f, CODE_MASK, CODE_EXP, ALU.bitwise_and, ALU.bitwise_or).then_inc(dq_bits, 1)

                def unit_clamp(g, n):
                    u, r = unit_index(g, n), n % 2
                    dve.wait_ge(dq_bits, u + 1)
                    dve.wait_ge(dq_value, START + at_least_0(u - 1))
                    dve.tensor_scalar(dq_g[:, r, :], dq_f[:, r, :], -0.25, 0.25, ALU.max, ALU.min).then_inc(dq_clamp, 1)

                def unit_value(g, n):
                    u, r = unit_index(g, n), n % 2
                    dve.wait_ge(dq_sum, START + u + 1)
                    dve.wait_ge(dq_sign, u + 1)
                    dve.wait_ge(dq_weight, START + at_least_0(u - 1))
                    dve.scalar_tensor_tensor(out=dq_c[:, r, :], in0=dq_c[:, r, :], scalar=-0.25, in1=dq_g[:, r, :],
                                             op0=ALU.mult, op1=ALU.add).then_inc(dq_value, 1)

                def unit_lo(g, n, k, gp):
                    u, r = unit_index(g, n), n % 2
                    dve.wait_ge(w_hi_made, u + 1)
                    hi, lo = weight_place(k, gp)
                    dve.tensor_tensor(lo, bank_w[r][:], f32(hi), ALU.subtract).then_inc(w_lo_made, 1)

                def elementwise_z(g, b, n):
                    e = (g * B + b) * NCH + n
                    dve.wait_ge(sq_made, e + 1)
                    dve.scalar_tensor_tensor(out=act_buf[n][:], in0=act_buf[n][:], scalar=1.0 / GELU_B,
                                             in1=bank_g[n][:], op0=ALU.add, op1=ALU.mult).then_inc(z_made, 1)

                def elementwise_v(g, b, n):
                    e = (g * B + b) * NCH + n
                    dve.wait_ge(tanh_made, e + 1)
                    dve.scalar_tensor_tensor(out=act_buf[n][:], in0=act_buf[n][:], scalar=1.0, in1=bank_g[n][:],
                                             op0=ALU.add, op1=ALU.mult).then_inc(a_made, 1)
                    dve.wait_ge(a_made, e + 1)
                    dve.scalar_tensor_tensor(out=act_buf[n][:], in0=act_buf[n][:], scalar=0.5, in1=bank_u[n][:],
                                             op0=ALU.mult, op1=ALU.mult).then_inc(v_made, 1)

                def elementwise_lo(g, b, n):
                    e = (g * B + b) * NCH + n
                    dve.wait_ge(in_hi_made, e + 1)
                    i = inter[b % 2]
                    dve.tensor_tensor(i[1][:, n, :], act_buf[n][:], f32(i[0][:, n, :]), ALU.subtract)\
                       .then_inc(in_lo_made, 1)

                def add_down(g, b, t):
                    s = g * B + b
                    dve.wait_ge(down_mm, START + s * NT + t + 1)
                    xt = x[:, b * NT + t, :]
                    dve.tensor_tensor(xt, bank_d[t % 2][:], xt, ALU.add).then_inc(down_added, 1)

                def codes_and_clamp(n):
                    unit_codes(0, n, ORDER[n])
                    unit_clamp(0, n)

                l3_stats(0)
                codes_and_clamp(0)
                l3_scale(0)
                codes_and_clamp(1)
                unit_value(0, 0)
                for t in range(NT):
                    l3_lo_tile(0, t, l3_bank[t])
                    if t == 1:
                        unit_value(0, 1)
                l3_stats(1)
                for n in range(NCH):
                    unit_lo(0, 2 * n, ORDER[2 * n], 0)
                    codes_and_clamp(2 * n + 2)
                    unit_lo(0, 2 * n + 1, ORDER[2 * n + 1], 0)
                    codes_and_clamp(2 * n + 3)
                    unit_value(0, 2 * n + 2)
                    if n == 0:
                        l3_scale(1)
                    unit_value(0, 2 * n + 3)
                    elementwise_z(0, 0, n)
                    if n == 0:
                        for t in range(NT):
                            l3_lo_tile(1, t, l3_bank[t])
                    elementwise_v(0, 0, n)
                    elementwise_lo(0, 0, n)
                for n in range(2 * NCH, UNITS):
                    unit_lo(0, n, ORDER[n], 0)

                def emit(g, gp, b, first_group, last_group):
                    nb = (b + 1) % B
                    ng = g if nb else g + 1
                    more = nb or not last_group
                    units = [] if last_group else [ORDER.index(k) for k in UNITS_AT[b]]
                    first, second = units_at(b, last_group)
                    if first_group and b + AHEAD < B:
                        l3_stats(b + AHEAD)
                    for n, transposed in enumerate((second, first)):
                        ln = first_group and b + AHEAD < B and n == 0
                        if n < len(units):
                            unit_codes(g + 1, units[n], ORDER[units[n]])
                        if ln:
                            l3_scale(b + AHEAD)
                        if more:
                            elementwise_z(ng, nb, n)
                        if transposed is not None:
                            unit_lo(g + 1, transposed, ORDER[transposed], 1 - gp)
                        for t in range(2):
                            if ln:
                                l3_lo_tile(b + AHEAD, t, bank_w[t])
                        if n < len(units):
                            unit_clamp(g + 1, units[n])
                        if more:
                            elementwise_v(ng, nb, n)
                        if n < len(units):
                            unit_value(g + 1, units[n])
                        if more:
                            elementwise_lo(ng, nb, n)
                        for t in range(2, NT):
                            if ln:
                                l3_lo_tile(b + AHEAD, t, bank_w[t % 2])
                        add_down(g, b, 2 * n)
                        add_down(g, b, 2 * n + 1)

                substeps(emit, dve)


_INS = ['x', 'ctx_1024', 'L0_attn_Wq', 'L0_attn_bq', 'L0_attn_Wk', 'L0_attn_bk', 'L0_attn_Wv', 'L0_attn_bv',
        'L0_attn_Wo', 'L0_attn_bo', 'L0_xattn_Wq', 'L0_xattn_bq', 'L0_xattn_Wk', 'L0_xattn_bk',
        'L0_ffn_gate_W_packed', 'L0_ffn_gate_scales', 'L0_ffn_up_W_packed', 'L0_ffn_up_scales',
        'L0_ffn_down_W_packed', 'L0_ffn_down_scales']


def kernel(**inputs):
    import numpy as _np
    import concourse.bacc as _bacc
    from concourse import mybir as _mybir
    from concourse.bass_utils import run_bass_kernel_spmd as _run

    nc = _bacc.Bacc("TRN2", target_bir_lowering=False, num_devices=1)
    arrays, args = {}, []
    for name in _INS:
        a = _np.ascontiguousarray(inputs[name])
        arrays[f"in_{name}_dram"] = a
        args.append(nc.dram_tensor(f"in_{name}_dram", a.shape, _mybir.dt.from_np(a.dtype), kind="ExternalInput").ap())
    out = nc.dram_tensor("out_0_dram", inputs["x"].shape, _mybir.dt.float32, kind="ExternalOutput").ap()
    decoder_layer(nc, *args, out)
    r = _run(nc, [arrays], core_ids=[0])
    return r.results[0]["out_0_dram"]
```

```python
from contextlib import ExitStack

import numpy as np

import concourse.bass as bass
from concourse import mybir

F32 = mybir.dt.float32
F32R = mybir.dt.float32r
I32 = mybir.dt.int32
ACT = mybir.ActivationFunctionType
ALU = mybir.AluOpType
AX = mybir.AxisListType

P = 128
EPS = 1e-5


def decoder_layer(nc, x_in, ctx_in, wq_in, bq_in, wk_in, bk_in, wv_in, bv_in, wo_in, bo_in, xwq_in, xbq_in, xwk_in,
                  xbk_in, gate_in, gate_s_in, up_in, up_s_in, down_in, down_s_in, out):
    B, S, D = x_in.shape
    C = ctx_in.shape[2]
    HD = wk_in.shape[1]
    H = wq_in.shape[1] // HD
    F = gate_in.shape[0]
    NT = S // P
    KC = D // P
    CC = C // P
    SCALE = float(1.0 / np.sqrt(np.float32(HD)))
    assert HD == P and S == 512 and D == S and NT == 4 and KC == 4 and H % 2 == 0

    TILES = (H + 1) * NT
    XH = H
    LN1, CTX, KEY, VALT, XQ, XK, VAL = 0, 4, 6, 7, 8, 9, 10
    ITEMS = 11
    SPLITS = ITEMS - 1
    LAST = H + 3
    LOOP0, LOOP1 = 4, H - 2

    NG = 256
    NCH = NG // P
    G = F // NG
    UNITS = 3 * NCH
    UNITS_AT = [[0, 2], [1, 3], [4, 5], []]
    ORDER = [u for at in UNITS_AT for u in at]
    BLK = 32
    assert G % 2 == 0 and B == 4

    def tiles_before(b, h, j=0):
        return b * TILES + h * NT + j

    ctx = ExitStack()
    with ctx:
        def sem(name):
            return ctx.enter_context(nc.semaphore(name))

        def keep(name, shape, dt=F32):
            return ctx.enter_context(nc.sbuf_tensor(name, shape, dt))

        psum = [ctx.enter_context(nc.psum_tensor(f"bank{n}", [P, 512], F32)) for n in range(8)]
        acc = psum[0:4]
        ps_s = psum[4:6]
        ps_t = psum[6]
        ps_qv = psum[7]

        x = keep("x", [P, B * NT, D])
        ident = keep("ident", [P, P])
        neg_half = keep("neg_half", [P, NT])
        zero_col = keep("zero_col", [P, NT])
        stats = keep("stats", [P, NT, 6])
        mv = keep("mv", [P, NT, 2])
        ve = keep("ve", [P, NT])
        rstd = keep("rstd", [P, NT])
        mean3 = keep("mean3", [P, B * NT])
        rstd3 = keep("rstd3", [P, B * NT])
        hn = keep("hn", [P, NT, D])
        packed = keep("packed", [P, 3, 512], I32)
        gate_s = keep("gate_s", [P, F // P, D // BLK])
        up_s = keep("up_s", [P, F // P, D // BLK])
        down_s = keep("down_s", [P, KC, F // BLK])

        x_loaded = [sem("x_first_loaded"), sem("x_rest_loaded")]
        small_loaded = sem("small_loaded")
        ctx_loaded = sem("ctx_loaded")
        wq_loaded = [sem(f"wq_loaded{n}") for n in range(2)]
        wo_loaded = [sem(f"wo_loaded{n}") for n in range(2)]
        packed_loaded = [sem(f"packed_loaded{n}") for n in range(2)]
        scales_loaded = sem("scales_loaded")
        const_made = sem("const_made")
        once_mm = sem("once_mm")
        once_hi = sem("once_hi")
        once_lo = sem("once_lo")
        ln_bn = sem("ln_bn")
        ln_mv = sem("ln_mv")
        ln_ve = sem("ln_ve")
        ln_rstd = sem("ln_rstd")
        h_ready = sem("h_ready")
        bo_added = sem("bo_added")
        held = sem("held")
        item_mm = sem("item_mm")
        item_pre = sem("item_pre")
        item_hi = sem("item_hi")
        item_lo = sem("item_lo")
        l2_mm = sem("l2_mm")
        l2_hi = sem("l2_hi")
        l2_lo = sem("l2_lo")
        l3_mm = sem("l3_mm")
        l3_hi = sem("l3_hi")
        l3_lo = sem("l3_lo")
        wq_hi_made = sem("wq_hi_made")
        wq_lo_made = sem("wq_lo_made")
        wo_hi_made = sem("wo_hi_made")
        wo_lo_made = sem("wo_lo_made")
        q_mm = sem("q_mm")
        q_hi_made = sem("q_hi_made")
        q_lo_made = sem("q_lo_made")
        s_mm = sem("s_mm")
        max_made = sem("max_made")
        exp_made = sem("exp_made")
        rsum_inv = sem("rsum_inv")
        p_normed = sem("p_normed")
        t_mm = sem("t_mm")
        pt_hi_made = sem("pt_hi_made")
        pt_lo_made = sem("pt_lo_made")
        pv_mm = sem("pv_mm")
        at_hi_made = sem("at_hi_made")
        at_lo_made = sem("at_lo_made")
        wo_mm = sem("wo_mm")
        acc_ready = sem("acc_ready")
        att_added = sem("att_added")
        xm_mm = sem("xm_mm")
        xm_added = sem("xm_added")
        scales_times4 = sem("scales_times4")
        dq_shift = sem("dq_shift")
        dq_bits = sem("dq_bits")
        dq_sign = sem("dq_sign")
        dq_clamp = sem("dq_clamp")
        dq_sum = sem("dq_sum")
        dq_value = sem("dq_value")
        dq_weight = sem("dq_weight")
        w_mm = sem("w_mm")
        w_hi_made = sem("w_hi_made")
        w_lo_made = sem("w_lo_made")
        gu_mm = sem("gu_mm")
        sq_made = sem("sq_made")
        z_made = sem("z_made")
        tanh_made = sem("tanh_made")
        a_made = sem("a_made")
        v_made = sem("v_made")
        in_hi_made = sem("in_hi_made")
        in_lo_made = sem("in_lo_made")
        down_mm = sem("down_mm")
        down_added = sem("down_added")
        stored = sem("stored")

        def mm3(pe, bank, w, m, start, stop):
            pe.matmul(bank, w[0], m[0], start=start, stop=False, skip_group_check=True)
            pe.matmul(bank, w[0], m[1], start=False, stop=False, skip_group_check=True)
            return pe.matmul(bank, w[1], m[0], start=False, stop=stop, skip_group_check=True)

        START = 1
        pe_started = (item_mm, l2_mm, l3_mm, acc_ready, xm_mm, pv_mm, wo_mm, s_mm, t_mm, q_mm, w_mm, down_mm)
        act_started = (item_hi, l2_hi, l3_hi, wq_hi_made, wo_hi_made, q_hi_made, at_hi_made, pt_hi_made, exp_made)
        dve_started = (item_lo, l2_lo, l3_lo, item_pre, xm_added, q_lo_made, at_lo_made, pt_lo_made, max_made,
                       p_normed, dq_shift,
                       dq_value, w_lo_made, v_made, in_lo_made, h_ready)
        pool_started = (wq_lo_made, wo_lo_made, dq_sum, dq_weight)

        def start(engine, sems):
            for s in sems:
                engine.sem_inc(s, START)

        def at_least_0(n):
            return max(n, 0) if isinstance(n, int) else n

        def hold(engine):
            engine.sem_inc(held, 1)

        def f32(ap):
            return ap.bitcast(F32)

        def stats_index(b, which, more=True):
            if which == 1:
                return 0 if isinstance(b, int) and b == 0 else b * 3 - 2
            return b * 3 + which if more else b * 3 + which - 1

        def ln_index(b, which):
            if which == 3:
                return 2 * B + b if b else 2 * B - 1
            if which == 2:
                return b * 2 + 2
            return 0 if isinstance(b, int) and b == 0 else b * 2 - 1

        def x_tile(b):
            return lambda t: x[:, b * NT + t, :]

        def layer_norm_stats(dve, n, xt, tiles=range(NT)):
            for t in tiles:
                dve.bn_stats(stats[:, t, :], xt(t)).then_inc(ln_bn, 1)

        def layer_norm_aggregate(dve, n):
            if not (isinstance(n, int) and n == 0):
                dve.wait_ge(ln_rstd, n)
            dve.wait_ge(ln_bn, n * NT + NT)
            hold(dve)
            for t in range(NT):
                dve.bn_aggr(mv[:, t, :], stats[:, t, :]).then_inc(ln_mv, 1)

        def layer_norm_scale(dve, n, xt):
            dve.wait_ge(ln_rstd, n + 1)
            for t in range(NT):
                dve.tensor_scalar(hn[:, t, :], xt(t), mv[:, t, 0:1], rstd[:, t:t + 1], ALU.subtract,
                                  ALU.mult).then_inc(h_ready, 1)

        def third_layernorm_scale(dve, b):
            dve.wait_ge(ln_rstd, stats_index(b, 3) + 1)
            for t in range(b * NT, (b + 1) * NT):
                dve.tensor_scalar(hn[:, t - b * NT, :], x[:, t, :], mean3[:, t:t + 1], rstd3[:, t:t + 1],
                                  ALU.subtract, ALU.mult).then_inc(h_ready, 1)

        def layer_norm_rstd(pool, n, keep_third=None):
            pool.wait_ge(ln_mv, n * NT + NT)
            hold(pool)
            pool.tensor_scalar(ve[:], mv[:, :, 1], EPS, None, ALU.add).then_inc(ln_ve, 1)
            pool.wait_ge(ln_ve, n + 1)
            if keep_third is None:
                pool.tensor_tensor(rstd[:], ve[:], neg_half[:], ALU.pow).then_inc(ln_rstd, 1)
            else:
                tiles = bass.ds(keep_third * NT, NT)
                pool.tensor_tensor(rstd3[:, tiles], ve[:], neg_half[:], ALU.pow)
                pool.tensor_tensor(mean3[:, tiles], mv[:, :, 0], zero_col[:], ALU.add).then_inc(ln_rstd, 1)

        gate_dram = gate_in.rearrange("(g n p) k -> p g n k", p=P, n=NCH)
        up_dram = up_in.rearrange("(g n p) k -> p g n k", p=P, n=NCH)
        down_dram = down_in.rearrange("(t p) (g k) -> p g t k", p=P, k=NG // 2)

        hT = keep("hT_hi", [P, KC, S], F32R), keep("hT_lo", [P, KC, S], F32R)
        h3T = [hT]
        wg0 = keep("wg0_hi", [P, NCH, KC, P], F32R), keep("wg0_lo", [P, NCH, KC, P], F32R)
        wu0 = keep("wu0_hi", [P, NCH, KC, P], F32R), keep("wu0_lo", [P, NCH, KC, P], F32R)
        wd0 = keep("wd0_hi", [P, NCH, D], F32R), keep("wd0_lo", [P, NCH, D], F32R)

        def load_codes(sp, g):
            sp.dma_start(packed[:, 0, :].rearrange("p (n k) -> p n k", n=NCH), gate_dram[:, g])\
              .then_inc(packed_loaded[0], 16)
            sp.dma_start(packed[:, 1, :].rearrange("p (n k) -> p n k", n=NCH), up_dram[:, g])\
              .then_inc(packed_loaded[0], 16)
            sp.dma_start(packed[:, 2, :].rearrange("p (t k) -> p t k", t=KC), down_dram[:, g])\
              .then_inc(packed_loaded[1], 16)

        CODE_MASK = np.int32(np.uint32(0x81C00000).view(np.int32)).item()
        CODE_EXP = 0x3E000000

        def unit_index(g, n):
            return g * UNITS + n

        def before(dq, u):
            return START + at_least_0(u - len(dq[0]) + 1)

        def unit_codes(dve, dq, g, n, k):
            u, f = unit_index(g, n), dq[0][n % len(dq[0])].bitcast(I32)
            if k < 2 * NCH:
                src = packed[:, k // NCH, (k % NCH) * 256:(k % NCH) * 256 + 256]
                dst = f.rearrange("p (k e) -> p k e", e=2)
                dve.wait_ge(packed_loaded[0], g * 32 + 32)
                parts = [(dst[:, :, e], src) for e in range(2)]
            else:
                j = k - 2 * NCH
                src = packed[:, 2, :].rearrange("p (t k) -> p t k", t=KC)[:, :, j * 64:(j + 1) * 64]
                dst = f.rearrange("p (t k e) -> p t k e", t=KC, e=2)
                dve.wait_ge(packed_loaded[1], g * 16 + 16)
                parts = [(dst[:, :, :, e], src) for e in range(2)]
            dve.wait_ge(dq_sum, before(dq, u))
            for e, (d, s) in enumerate(parts):
                dve.tensor_scalar(d, s, 28 - 4 * e, 6, ALU.logical_shift_left, ALU.arith_shift_right)\
                   .then_inc(dq_shift, 1)
            dve.wait_ge(dq_shift, START + u * 2 + 2)
            dve.tensor_scalar(f, f, CODE_MASK, CODE_EXP, ALU.bitwise_and, ALU.bitwise_or).then_inc(dq_bits, 1)

        def unit_sign(act, dq, g, n):
            u, r = unit_index(g, n), n % len(dq[0])
            act.wait_ge(dq_bits, u + 1)
            act.wait_ge(dq_weight, before(dq, u))
            act.activation(dq[2][r], dq[0][r], ACT.Sign).then_inc(dq_sign, 1)

        def unit_clamp(dve, dq, g, n):
            u, r = unit_index(g, n), n % len(dq[0])
            dve.wait_ge(dq_bits, u + 1)
            dve.wait_ge(dq_value, before(dq, u))
            dve.tensor_scalar(dq[1][r], dq[0][r], -0.25, 0.25, ALU.max, ALU.min).then_inc(dq_clamp, 1)

        def unit_sum(pool, dq, g, n):
            u, r = unit_index(g, n), n % len(dq[0])
            pool.wait_ge(dq_clamp, u + 1)
            pool.tensor_tensor(dq[1][r], dq[1][r], dq[0][r], ALU.add).then_inc(dq_sum, 1)

        def unit_value(dve, dq, g, n):
            u, r = unit_index(g, n), n % len(dq[0])
            dve.wait_ge(dq_sum, START + u + 1)
            dve.wait_ge(dq_sign, u + 1)
            dve.wait_ge(dq_weight, before(dq, u))
            dve.scalar_tensor_tensor(out=dq[2][r], in0=dq[2][r], scalar=-0.25, in1=dq[1][r],
                                     op0=ALU.mult, op1=ALU.add).then_inc(dq_value, 1)

        def unit_weight(pool, dq, g, n, k):
            u, r = unit_index(g, n), n % len(dq[0])
            pool.wait_ge(dq_value, START + u + 1)
            pool.wait_ge(w_mm, before(dq, u))
            if k < 2 * NCH:
                sc = (gate_s, up_s)[k // NCH][:, bass.ds(g * NCH + k % NCH, 1), :]\
                    .rearrange("p a k -> p (a k)").unsqueeze(2).to_broadcast([P, D // BLK, BLK])
                ins = pool.tensor_tensor(dq[3][r].rearrange("p (k e) -> p k e", e=BLK),
                                         dq[2][r].rearrange("p (k e) -> p k e", e=BLK), sc, ALU.mult)
            else:
                j = k - 2 * NCH
                sc = down_s[:, :, bass.ds(g * (NG // BLK) + j * (P // BLK), P // BLK)]\
                    .unsqueeze(3).to_broadcast([P, KC, P // BLK, BLK])
                ins = pool.tensor_tensor(dq[3][r].rearrange("p (t k e) -> p t k e", t=KC, e=BLK),
                                         dq[2][r].rearrange("p (t k e) -> p t k e", t=KC, e=BLK), sc, ALU.mult)
            ins.then_inc(dq_weight, 1)

        def unit_transpose(pe, dq, bank, g, n):
            u, r = unit_index(g, n), n % len(dq[0])
            pe.wait_ge(dq_weight, START + u + 1)
            for c in range(KC):
                mm = pe.transpose(bank[:, c * P:(c + 1) * P], dq[3][r][:, c * P:(c + 1) * P], ident[:])
            mm.then_inc(w_mm, 1)

        def weight_place(sets, k):
            pairs = sets[k // NCH]
            if k < 2 * NCH:
                return [w[:, k % NCH].rearrange("p c n -> p (c n)") for w in pairs]
            return [w[:, k - 2 * NCH, :] for w in pairs]

        def unit_hi(act, sets, bank, g, n, k):
            act.wait_ge(w_mm, START + unit_index(g, n) + 1)
            if n == 0 and not (isinstance(g, int) and g == 0):
                act.wait_ge(down_mm, START + (g - 1) * (B * NT))
            act.activation(weight_place(sets, k)[0], bank[:], ACT.Copy).then_inc(w_hi_made, 1)

        def unit_lo(dve, sets, bank, g, n, k):
            dve.wait_ge(w_hi_made, unit_index(g, n) + 1)
            hi, lo = weight_place(sets, k)
            dve.tensor_tensor(lo, bank[:], f32(hi), ALU.subtract).then_inc(w_lo_made, 1)

        def l3_transpose(pe, b, t, bank):
            pe.wait_ge(h_ready, START + ln_index(b, 3) * NT + t + 1)
            for c in range(KC):
                mm = pe.transpose(bank[:, c * P:(c + 1) * P], hn[:, t, c * P:(c + 1) * P], ident[:])
            mm.then_inc(l3_mm, 1)

        def l3_hi_tile(act, b, t, bank):
            act.wait_ge(l3_mm, START + b * NT + t + 1)
            act.activation(h3T[b][0][:, :, t * P:(t + 1) * P], bank[:].rearrange("p (c n) -> p c n", c=KC),
                           ACT.Copy).then_inc(l3_hi, 1)

        def l3_lo_tile(dve, b, t, bank):
            dve.wait_ge(l3_hi, START + b * NT + t + 1)
            cols = slice(t * P, (t + 1) * P)
            dve.tensor_tensor(h3T[b][1][:, :, cols], bank[:].rearrange("p (c n) -> p c n", c=KC),
                              f32(h3T[b][0][:, :, cols]), ALU.subtract).then_inc(l3_lo, 1)

        def gate_up_products(pe, sets, banks, b, n):
            for w, bank in zip(sets, banks):
                for c in range(KC):
                    mm = mm3(pe, bank[:], (w[0][:, n, c, :], w[1][:, n, c, :]),
                             (h3T[b][0][:, c, :], h3T[b][1][:, c, :]), c == 0, c == KC - 1)
                mm.then_inc(gu_mm, 1)

        ahead_banks = psum[4:6]

        with ExitStack() as att:
            def sb(name, shape, dt=F32):
                return att.enter_context(nc.sbuf_tensor(name, shape, dt))

            def pair(name, shape):
                return sb(name + "_hi", shape, F32R), sb(name + "_lo", shape, F32R)

            kT = pair("kT", [P, S])
            v = pair("v", [P, NT, HD])
            wkv_p = wg0
            bq = sb("bq", [P, H])
            bk = sb("bk", [P, 1])
            bv = sb("bv", [P, 1])
            bo = sb("bo", [P, D])
            xbq = sb("xbq", [P, 1])
            xbk = sb("xbk", [P, 1])
            xwT = [wu0[0][:, n].rearrange("p (a c) d -> p a c d", a=2) for n in range(2)]
            ctx_sb = sb("ctx_sb", [P, NT, C])
            ctxT = wd0
            kf = ctx_sb[:, 0:2, :].rearrange("p t c -> p (t c)")
            vf = ctx_sb[:, 2:4, :].rearrange("p t c -> p (t c)")
            xq = pair("xq", [P, S])
            xk = pair("xk", [P, S])
            zeros = sb("zeros", [P, S], F32R)
            wq_st = sb("wq_st", [P, 2, KC, HD])
            wo_st = sb("wo_st", [P, 2, D])
            wq = [pair(f"wq{n}", [P, KC, HD]) for n in range(2)]
            wo = [pair(f"wo{n}", [P, D]) for n in range(2)]
            q = [pair(f"q{n}", [P, S]) for n in range(2)]
            prob = sb("prob", [P, 2, NT, S])
            wkv = prob[:, 0, 0:2, :].rearrange("p a (c d) -> p a c d", c=KC)
            xw = prob[:, 1, 0, :].rearrange("p (a c) -> p a c", a=2)
            neg_max = sb("neg_max", [P, 2, NT])
            rsum = sb("rsum", [P, 2, NT])
            rinv = sb("rinv", [P, 2, NT])
            pT = [pair(f"pT{n}", [P, NT, S]) for n in range(2)]
            at = [pair(f"at{n}", [P, S]) for n in range(2)]
            l2T = pT[(H - 1) % 2]
            xpT = pT[XH % 2]

            wq_dram = wq_in.rearrange("(c p) (h d) -> p c h d", p=P, d=HD)
            wo_dram = wo_in.rearrange("(h d) n -> d h n", d=HD)
            ctx_dram = ctx_in.rearrange("b (t p) c -> b p t c", p=P)
            x_dram = x_in.rearrange("b (t p) n -> b p t n", p=P)
            SMALL_LOADS = 11

            def at_work(i, lag, n):
                return not isinstance(i, int) or 0 <= i - lag < n

            def last_use(b, per, h):
                return START + b * per + at_least_0(h - 1) * (per // H)

            ITEM_AT = {(H, 2): 0, (H, 3): 1, (H + 1, 2): 2, (H + 1, 3): 3, (H + 2, 0): CTX, (H + 2, 1): CTX + 1,
                       (H + 2, 2): KEY}
            ITEMS_AFTER = (VALT, XQ, XK, VAL)
            ITEM_BANK = [ps_qv] * 4 + [ps_s[0], ps_s[1], ps_qv, ps_qv, ps_s[0], ps_s[1], ps_t]
            HALVES = (0, 1), (2, 3)
            UNIT0 = H - UNITS
            assert (UNIT0 - LOOP0) % 2 == 0
            hn_dq = [[hn[:, n, :]] for n in range(4)]
            first_sets = (wg0, wu0, wd0)

            def item_at(i, j):
                return ITEM_AT.get((i, j)) if isinstance(i, int) else None

            def l3_at(i, j, more):
                n = item_at(i, j)
                return n if not more and n in range(CTX) else None

            def unit_at(i, more):
                return i - UNIT0 if not more and isinstance(i, int) and 0 <= i - UNIT0 < UNITS else None

            def split_count(b, n):
                return START + b * SPLITS + (n + 1 if n < VALT else n)

            def pipeline(engine, b, iteration, more):
                loop1 = LOOP1 if more else UNIT0
                for i in range(2, LOOP0):
                    iteration(b, i, i % 2, more)
                with engine.Fori(0, (loop1 - LOOP0) // 2) as n:
                    for par in range(2):
                        iteration(b, n * 2 + (LOOP0 + par), par, more)
                for i in range(loop1, LAST + 1):
                    iteration(b, i, i % 2, more)

            def batches(engine, batch):
                with engine.Fori(0, B - 1) as b:
                    batch(b, True)
                batch(B - 1, False)

            blk = att.enter_context(nc.Block())

            @blk.sync
            def _(sp):
                def load_x(b):
                    sp.dma_start(x[:, b * NT:(b + 1) * NT, :], x_dram[b]).then_inc(x_loaded[min(b, 1)], 16)

                load_x(0)
                with nc.allow_non_contiguous_dma(reason="biases as columns, once"):
                    for dst, src in (
                        (wkv[:, 0], wk_in.rearrange("(c p) d -> p c d", p=P)),
                        (wkv[:, 1], wv_in.rearrange("(c p) d -> p c d", p=P)),
                        (xw[:, 0, :], xwq_in), (xw[:, 1, :], xwk_in),
                        (bk[:], bk_in.rearrange("(p a) -> p a", a=1)),
                        (xbq[:], xbq_in.rearrange("(p a) -> p a", a=1)),
                        (xbk[:], xbk_in.rearrange("(p a) -> p a", a=1)),
                        (bv[:], bv_in.rearrange("(p a) -> p a", a=1)),
                        (bo[:], bo_in.partition_broadcast(P)),
                    ):
                        sp.dma_start(dst, src).then_inc(small_loaded, 16)
                    for n in range(2):
                        half = slice(n * H // 2, (n + 1) * H // 2)
                        sp.dma_start(bq[:, half], bq_in.rearrange("(h d) -> d h", d=HD)[:, half])\
                          .then_inc(small_loaded, 16)
                sp.dma_start(ctx_sb[:], ctx_dram[0]).then_inc(ctx_loaded, 16)

                def load_wq(b, h, p, wrap=0):
                    sp.wait_ge(wq_lo_made, last_use(b, H, h))
                    sp.dma_start(wq_st[:, p], wq_dram[:, :, h - wrap, :]).then_inc(wq_loaded[p], 16)

                def iteration(b, i, par, more):
                    if at_work(i, -2, H):
                        load_wq(b, i + 2, par)
                    elif more and i + 2 < H + 2:
                        load_wq(b, i + 2, par, H)
                    if at_work(i, 1, H):
                        p = 1 - par
                        sp.wait_ge(wo_lo_made, last_use(b, H, i - 1))
                        sp.dma_start(wo_st[:, p], wo_dram[:, i - 1, :]).then_inc(wo_loaded[p], 16)

                for i in (-2, -1):
                    iteration(0, i, i % 2, True)
                for b in range(1, B):
                    load_x(b)
                for i in (0, 1):
                    iteration(0, i, i % 2, True)

                def batch(b, more):
                    if not more:
                        with nc.allow_non_contiguous_dma(reason="scales"):
                            for dst, src in ((gate_s, gate_s_in), (up_s, up_s_in), (down_s, down_s_in)):
                                sp.dma_start(dst[:], src.rearrange("(n p) k -> p n k", p=P))\
                                  .then_inc(scales_loaded, 16)
                        load_codes(sp, 0)
                    if more:
                        sp.wait_ge(item_lo, split_count(b, VAL))
                        sp.dma_start(ctx_sb[:], ctx_dram[b + 1]).then_inc(ctx_loaded, 16)
                    pipeline(sp, b, iteration, more)
                    if more:
                        for i in (0, 1):
                            iteration(b + 1, i, i % 2, True)

                batches(sp, batch)

            @blk.gpsimd
            def _(pool):
                start(pool, pool_started)
                pool.memset(ident[:], 0.0).then_inc(const_made, 1)
                pool.wait_ge(const_made, 1)
                pool.affine_select(out=ident[:], in_=ident[:], compare_op=ALU.not_equal, fill=1.0, base=0,
                                   pattern=[[-1, P]], channel_multiplier=1).then_inc(const_made, 1)
                pool.memset(neg_half[:], -0.5).then_inc(const_made, 1)
                pool.memset(zero_col[:], 0.0).then_inc(const_made, 1)
                pool.wait_ge(const_made, 4)

                def add_bo(b, t):
                    pool.wait_ge(h_ready, START + ln_index(b, 1) * NT + t + 1)
                    pool.tensor_tensor(x[:, b * NT + t, :], x[:, b * NT + t, :], bo[:], ALU.add)\
                        .then_inc(bo_added, 1)

                def iteration(b, i, par, more):
                    p = 1 - par
                    unit = unit_at(i, more)
                    if at_work(i, -1, H) or (more and i == H - 1):
                        pool.wait_ge(wq_hi_made, START + b * H + i + 2)
                        pool.tensor_tensor(wq[p][1][:], wq_st[:, p], f32(wq[p][0][:]), ALU.subtract)\
                            .then_inc(wq_lo_made, 1)
                    if at_work(i, 3, H):
                        if unit is not None:
                            unit_sum(pool, hn_dq, 0, unit)
                        pool.wait_ge(wo_hi_made, START + b * H + i - 2)
                        pool.tensor_tensor(wo[p][1][:], wo_st[:, p], f32(wo[p][0][:]), ALU.subtract)\
                            .then_inc(wo_lo_made, 1)
                    if unit is not None:
                        if unit == 0:
                            pool.wait_ge(scales_times4, 3)
                        unit_weight(pool, hn_dq, 0, unit, ORDER[unit])
                    if more and isinstance(i, int) and i == H - 2:
                        layer_norm_rstd(pool, stats_index(b + 1, 1))
                    if more and isinstance(i, int) and H <= i < H + NT:
                        add_bo(b + 1, i - H)

                layer_norm_rstd(pool, 0)
                iteration(0, -1, 1, True)
                pool.wait_ge(small_loaded, 16 * SMALL_LOADS)
                for t in range(NT):
                    add_bo(0, t)
                for i in (0, 1):
                    iteration(0, i, i % 2, True)

                def batch(b, more):
                    pipeline(pool, b, iteration, more)
                    layer_norm_rstd(pool, stats_index(b, 2, more))
                    if more:
                        for i in (0, 1):
                            iteration(b + 1, i, i % 2, True)
                        layer_norm_rstd(pool, stats_index(b, 3), keep_third=b)

                batches(pool, batch)

            @blk.tensor
            def _(pe):
                start(pe, pe_started)
                pe.wait_ge(const_made, 3)
                pe.wait_ge(small_loaded, 16 * SMALL_LOADS)
                for n in range(2):
                    for c in range(CC):
                        mm = pe.transpose(ps_qv[:, (n * CC + c) * P:(n * CC + c + 1) * P],
                                          xw[:, n, c * P:(c + 1) * P], ident[:])
                mm.then_inc(once_mm, 1)

                def item(b, n, bank):
                    if n < CTX:
                        pe.wait_ge(h_ready, START + ln_index(b, 1) * NT + n + 1)
                        for c in range(KC):
                            mm = pe.transpose(bank[:, c * P:(c + 1) * P], hn[:, n, c * P:(c + 1) * P], ident[:])
                    elif n < KEY:
                        pe.wait_ge(ctx_loaded, b * 16 + 16)
                        for m in range(2):
                            for c in range(CC):
                                mm = pe.transpose(bank[:, (m * CC + c) * P:(m * CC + c + 1) * P],
                                                  ctx_sb[:, 2 * (n - CTX) + m, c * P:(c + 1) * P], ident[:])
                    elif n == KEY:
                        pe.wait_ge(item_lo, split_count(b, LN1 + NT - 1))
                        for c in range(KC):
                            mm = mm3(pe, bank[:], (wkv_p[0][:, 0, c, :], wkv_p[1][:, 0, c, :]),
                                     (hT[0][:, c, :], hT[1][:, c, :]), c == 0, c == KC - 1)
                    elif n == VALT:
                        pe.wait_ge(item_pre, START + b * 2 + 1)
                        for c in range(KC):
                            mm = mm3(pe, bank[:], (wkv_p[0][:, 1, c, :], wkv_p[1][:, 1, c, :]),
                                     (hT[0][:, c, :], hT[1][:, c, :]), c == 0, c == KC - 1)
                    elif n == VAL:
                        pe.wait_ge(item_pre, START + b * 2 + 2)
                        pe.wait_ge(pt_lo_made, START + b * TILES)
                        for t in range(NT):
                            mm = pe.transpose(bank[:, t * P:(t + 1) * P], vf[:, t * P:(t + 1) * P], ident[:])
                    else:
                        pe.wait_ge(item_lo, split_count(b, CTX + 1))
                        for c in range(CC):
                            mm = mm3(pe, bank[:], (xwT[0][:, n - XQ, c, :], xwT[1][:, n - XQ, c, :]),
                                     (ctxT[0][:, c, :], ctxT[1][:, c, :]), c == 0, c == CC - 1)
                    mm.then_inc(item_mm, 1)

                def item_in_pipeline(b, i, n):
                    if n in (0, 2, KEY):
                        pe.wait_ge(at_lo_made, START + b * H + i - 2)
                    elif n in (1, 3):
                        pe.wait_ge(item_lo, split_count(b + 1, n - 1))
                    elif n in (CTX, CTX + 1):
                        pe.wait_ge(exp_made, START + tiles_before(b, XH, 3 + n - CTX))
                    item(b + 1, n, ITEM_BANK[n])

                def queries(b, i, par, chunks):
                    if 0 in chunks:
                        pe.wait_ge(wq_lo_made, START + b * H + i + 1)
                        if isinstance(i, int) and i == 0:
                            pe.wait_ge(item_pre, START + b * 2 + 2)
                        elif isinstance(i, int) and i < 3:
                            pe.wait_ge(q_lo_made, START + b * H + i)
                        else:
                            pe.wait_ge(at_lo_made, START + b * H + i - 2)
                    for c in chunks:
                        mm = mm3(pe, ps_qv[:], (wq[par][0][:, c, :], wq[par][1][:, c, :]),
                                 (hT[0][:, c, :], hT[1][:, c, :]), c == 0, c == KC - 1)
                    if KC - 1 in chunks:
                        mm.then_inc(q_mm, 1)

                def cross_product(b, t):
                    if t == 0:
                        pe.wait_ge(l2_lo, START + b * NT + NT)
                    for c in range(KC):
                        mm = mm3(pe, acc[t][:], (l2T[0][:, c, t * P:(t + 1) * P], l2T[1][:, c, t * P:(t + 1) * P]),
                                 (xpT[0][:, c, :], xpT[1][:, c, :]), c == 0, c == KC - 1)
                    mm.then_inc(xm_mm, 1)

                def project(b, i, par, j):
                    h, p = i - 4, par
                    if j == 0:
                        pe.wait_ge(wo_lo_made, START + b * H + h + 1)
                        pe.wait_ge(at_lo_made, START + b * H + h + 1)
                    last = isinstance(i, int) and h == H - 1
                    mm = mm3(pe, acc[j][:], (at[p][0][:, j * P:(j + 1) * P], at[p][1][:, j * P:(j + 1) * P]),
                             (wo[p][0][:], wo[p][1][:]), False, last)
                    if last:
                        mm.then_inc(acc_ready, 1)
                    elif j == NT - 1:
                        mm.then_inc(wo_mm, 1)

                def iteration(b, i, par, more):
                    for j in range(NT):
                        if at_work(i, 2, H + 1):
                            h, p = i - 2, par
                            pe.wait_ge(p_normed, START + tiles_before(b, h, j + 1))
                            pe.wait_ge(pt_lo_made, START + tiles_before(b, h, j))
                            for c in range(NT):
                                mm = pe.transpose(ps_t[:, c * P:(c + 1) * P], prob[:, p, j, c * P:(c + 1) * P],
                                                  ident[:])
                            mm.then_inc(t_mm, 1)
                        if j == 0 and at_work(i, 4, H):
                            project(b, i, par, 0)
                        if j < 2 and at_work(i, 3, H):
                            h, p = i - 3, 1 - par
                            if j == 0:
                                pe.wait_ge(pt_lo_made, START + tiles_before(b, h, NT))
                                if isinstance(i, int) and i > H:
                                    if more:
                                        pe.wait_ge(item_lo, split_count(b + 1, 2 * (i - H) - 1))
                                    else:
                                        pe.wait_ge(l3_lo, START + 2 * (i - H))
                                else:
                                    pe.wait_ge(q_lo_made, START + b * H + i)
                            for c in (2 * j, 2 * j + 1):
                                mm = mm3(pe, ps_qv[:], (v[0][:, c, :], v[1][:, c, :]),
                                         (pT[p][0][:, c, :], pT[p][1][:, c, :]), c == 0, c == NT - 1)
                            if j:
                                mm.then_inc(pv_mm, 1)
                        if j >= 2 and at_work(i, 0, H):
                            queries(b, i, par, HALVES[j - 2])
                        if more and item_at(i, j) is not None:
                            item_in_pipeline(b, i, item_at(i, j))
                        if l3_at(i, j, more) is not None:
                            n = l3_at(i, j, more)
                            if n % 2 == 0:
                                pe.wait_ge(at_lo_made, START + b * H + i - 2)
                            else:
                                pe.wait_ge(l3_lo, START + n)
                            l3_transpose(pe, 0, n, ps_qv)
                        if j == 0 and unit_at(i - 1, more) is not None:
                            pe.wait_ge(w_lo_made, START + unit_at(i - 1, more) + 1)
                        if at_work(i, 1, H + 1):
                            scores(b, i - 1, 1 - par, j)
                        if j > 0 and at_work(i, 4, H):
                            project(b, i, par, j)
                    if unit_at(i, more) is not None:
                        pe.wait_ge(exp_made, START + tiles_before(b, i - 1, NT - 1))
                        unit_transpose(pe, hn_dq, ps_s[0], 0, unit_at(i, more))
                    if isinstance(i, int) and i == LOOP0 - 1:
                        pe.wait_ge(xm_added, START + b * NT)
                        for t in range(NT):
                            pe.matmul(acc[t][:], zeros[:, 0:P], zeros[:], start=True, stop=False,
                                      skip_group_check=True)

                def scores(b, h, p, j):
                    cross = isinstance(h, int) and h == XH
                    if j == 0 and not cross:
                        pe.wait_ge(q_lo_made, START + b * H + h + 1)
                    if isinstance(h, int) and h == 0:
                        pe.wait_ge(item_lo, split_count(b, VAL))
                    if j > 1 or not (isinstance(h, int) and h == 0):
                        pe.wait_ge(exp_made, START - 1 + tiles_before(b, h, j))
                    qq, kk = (xq, xk) if cross else (q[p], kT)
                    mm3(pe, ps_s[j % 2][:], (qq[0][:, j * P:(j + 1) * P], qq[1][:, j * P:(j + 1) * P]),
                        (kk[0][:], kk[1][:]), True, True).then_inc(s_mm, 1)

                def second_layernorm(b, more):
                    for t in range(NT):
                        pe.wait_ge(h_ready, START + ln_index(b, 2) * NT + t + 1)
                        for c in range(KC):
                            mm = pe.transpose(acc[t][:, c * P:(c + 1) * P], hn[:, t, c * P:(c + 1) * P], ident[:])
                        mm.then_inc(l2_mm, 1)

                def first_heads(b, before):
                    if before:
                        second_layernorm(b - 1, True)
                    queries(b, 0, 0, HALVES[0] + HALVES[1])
                    for j in range(NT):
                        if before:
                            cross_product(b - 1, j)
                        if j >= 2:
                            queries(b, 1, 1, HALVES[j - 2])
                        scores(b, 0, 0, j)

                for n in range(ITEMS):
                    if n == KEY:
                        pe.wait_ge(once_lo, 3)
                    item(0, n, acc[n] if n < CTX else ITEM_BANK[n])
                first_heads(0, False)

                def batch(b, more):
                    pipeline(pe, b, iteration, more)
                    if more:
                        for n in ITEMS_AFTER:
                            item(b + 1, n, ITEM_BANK[n])
                        first_heads(b + 1, True)
                    else:
                        pe.wait_ge(w_lo_made, START + 2)
                        pe.wait_ge(l3_lo, START + NT)
                        pe.wait_ge(exp_made, START + b * TILES + TILES)
                        gate_up_products(pe, first_sets[:2], ahead_banks, 0, 0)
                        second_layernorm(b, more)
                        for t in range(NT):
                            cross_product(b, t)

                batches(pe, batch)

            @blk.scalar
            def _(act):
                start(act, act_started)
                act.wait_ge(small_loaded, 16 * SMALL_LOADS)
                act.activation(wkv_p[0][:], wkv, ACT.Copy).then_inc(once_hi, 1)
                act.wait_ge(once_mm, 1)
                act.activation(xwT[0].rearrange("p a c d -> p (a c d)"), ps_qv[:], ACT.Copy).then_inc(once_hi, 1)

                def item_hi_part(b, n, bank):
                    if n == VALT:
                        return
                    if n == KEY:
                        act.wait_ge(item_pre, START + b * 2 + 1)
                        act.activation(kT[0][:], kf, ACT.Copy).then_inc(item_hi, 1)
                        return
                    act.wait_ge(item_mm, START + b * ITEMS + n + 1)
                    if n < CTX:
                        act.activation(hT[0][:, :, n * P:(n + 1) * P], bank[:].rearrange("p (c n) -> p c n", c=KC),
                                       ACT.Copy).then_inc(item_hi, 1)
                    elif n < KEY:
                        m = n - CTX
                        act.activation(ctxT[0][:, :, 2 * m * P:(2 * m + 2) * P].rearrange("p c (m n) -> p m c n", m=2),
                                       bank[:].rearrange("p (m c n) -> p m c n", m=2, c=CC), ACT.Copy)\
                           .then_inc(item_hi, 1)
                    elif n == VAL:
                        act.activation(v[0][:].rearrange("p t d -> p (t d)"), bank[:], ACT.Copy).then_inc(item_hi, 1)
                    else:
                        dst, bias = ((xq, xbq), (xk, xbk))[n - XQ]
                        act.activation(dst[0][:], bank[:], ACT.Identity, bias=bias[:]).then_inc(item_hi, 1)

                def query_hi(b, i, par):
                    act.wait_ge(q_mm, START + b * H + i + 1)
                    act.wait_ge(s_mm, START + b * TILES + at_least_0(i - 1) * NT)
                    act.activation(q[par][0][:], ps_qv[:], ACT.Identity, bias=bq[:, bass.ds(i, 1)])\
                       .then_inc(q_hi_made, 1)

                def exponentials(b, h, p, j):
                    act.wait_ge(max_made, START + tiles_before(b, h, j + 1))
                    act.wait_ge(t_mm, START + b * TILES + (0 if isinstance(h, int) and h < 2
                                                           else (h - 2) * NT + j + 1))
                    act.activation(prob[:, p, j, :], ps_s[j % 2][:], ACT.Exp, bias=neg_max[:, p, j:j + 1],
                                   accum_out=rsum[:, p, j:j + 1]).then_inc(exp_made, 1)

                def wait_loaded(loaded, b, h, p):
                    act.wait_ge(loaded, b * (8 * H) + h * 8 + (16 - 8 * p))

                def query_weights_hi(b, h, p):
                    wait_loaded(wq_loaded[p], b, h, p)
                    act.wait_ge(q_mm, last_use(b, H, h))
                    act.activation(wq[p][0][:], wq_st[:, p], ACT.Copy).then_inc(wq_hi_made, 1)

                def iteration(b, i, par, more):
                    for j in range(NT):
                        if j == 0 and unit_at(i - 1, more) is not None:
                            n = unit_at(i - 1, more)
                            unit_hi(act, first_sets, ps_s[0], 0, n, ORDER[n])
                        if at_work(i, 2, H + 1):
                            h, p = i - 2, par
                            act.wait_ge(t_mm, START + tiles_before(b, h, j + 1))
                            if j == 0:
                                act.wait_ge(pv_mm, last_use(b, H, h))
                                if isinstance(h, int) and h < 2:
                                    act.wait_ge(xm_mm, START + b * NT)
                            act.activation(pT[p][0][:, :, j * P:(j + 1) * P],
                                           ps_t[:].rearrange("p (c n) -> p c n", c=NT), ACT.Copy)\
                               .then_inc(pt_hi_made, 1)
                        if l3_at(i, j, more) is not None:
                            l3_hi_tile(act, 0, l3_at(i, j, more), ps_qv)
                        if more and item_at(i, j) in range(CTX):
                            item_hi_part(b + 1, item_at(i, j), ITEM_BANK[item_at(i, j)])
                        if j == 0 and at_work(i, 2, H + 1):
                            exponentials(b, i - 2, par, NT - 1)
                        if j > 0 and at_work(i, 1, H + 1):
                            exponentials(b, i - 1, 1 - par, j - 1)
                        if j == 1 and at_work(i, 3, H):
                            h, p = i - 3, 1 - par
                            act.wait_ge(pv_mm, START + b * H + h + 1)
                            act.wait_ge(wo_mm, START + b * (H - 1) + at_least_0(h - 1))
                            if isinstance(h, int) and h < 2:
                                act.wait_ge(acc_ready, START + b * NT)
                            act.activation(at[p][0][:], ps_qv[:], ACT.Copy).then_inc(at_hi_made, 1)
                        if j == NT - 1 and at_work(i, 0, H):
                            query_hi(b, i, par)
                        if more and item_at(i, j) in range(CTX, ITEMS):
                            item_hi_part(b + 1, item_at(i, j), ITEM_BANK[item_at(i, j)])
                        if j == 0 and (at_work(i, -1, H) or (more and i == H - 1)):
                            query_weights_hi(b, i + 1, 1 - par)
                        if j == (0 if isinstance(i, int) and i == LAST - 1 else 2) and at_work(i, 3, H):
                            h, p = i - 3, 1 - par
                            wait_loaded(wo_loaded[p], b, h, p)
                            act.wait_ge(wo_mm, START + b * (H - 1) + at_least_0(h - 1))
                            if isinstance(h, int) and h < 2:
                                act.wait_ge(acc_ready, START + b * NT)
                            act.activation(wo[p][0][:], wo_st[:, p], ACT.Copy).then_inc(wo_hi_made, 1)
                        if j == 1 and unit_at(i, more) is not None:
                            unit_sign(act, hn_dq, 0, unit_at(i, more))
                    if not more and isinstance(i, int) and i == LOOP0 - 1:
                        act.wait_ge(scales_loaded, 48)
                        for s in (gate_s, up_s, down_s):
                            act.activation(s[:], s[:], ACT.Copy, scale=4.0).then_inc(scales_times4, 1)

                def second_layernorm_hi(b):
                    act.wait_ge(pv_mm, START + b * H + H)
                    for t in range(NT):
                        act.wait_ge(l2_mm, START + b * NT + t + 1)
                        act.activation(l2T[0][:, :, t * P:(t + 1) * P], acc[t][:].rearrange("p (c n) -> p c n", c=KC),
                                       ACT.Copy).then_inc(l2_hi, 1)

                def first_heads(b, before):
                    if before:
                        second_layernorm_hi(b - 1)
                    query_hi(b, 0, 0)
                    query_weights_hi(b, 1, 1)
                    for j in range(NT):
                        if j > 0:
                            exponentials(b, 0, 0, j - 1)
                        if j == NT - 1:
                            query_hi(b, 1, 1)
                        if j == 0:
                            query_weights_hi(b, 2, 0)

                query_weights_hi(0, 0, 0)
                for n in range(ITEMS):
                    item_hi_part(0, n, acc[n] if n < CTX else ITEM_BANK[n])
                first_heads(0, False)

                def batch(b, more):
                    pipeline(act, b, iteration, more)
                    if more:
                        for n in ITEMS_AFTER:
                            item_hi_part(b + 1, n, ITEM_BANK[n])
                        first_heads(b + 1, True)
                    else:
                        second_layernorm_hi(b)

                batches(act, batch)

            @blk.vector
            def _(dve):
                start(dve, dve_started)
                dve.memset(f32(zeros[:]), 0.0).then_inc(once_lo, 1)

                def item_pre_part(b, n, bank):
                    dve.wait_ge(item_mm, START + b * ITEMS + n + 1)
                    if n == KEY:
                        dve.tensor_scalar(kf, bank[:], bk[:], SCALE, ALU.add, ALU.mult).then_inc(item_pre, 1)
                    else:
                        dve.tensor_scalar(vf, bank[:], bv[:], None, ALU.add).then_inc(item_pre, 1)

                def item_lo_part(b, n, bank, pre=True):
                    if pre and n in (KEY, VALT):
                        item_pre_part(b, n, bank)
                    if n == VALT:
                        return
                    dve.wait_ge(item_hi, split_count(b, n))
                    if n < CTX:
                        cols = slice(n * P, (n + 1) * P)
                        ins = dve.tensor_tensor(hT[1][:, :, cols], bank[:].rearrange("p (c n) -> p c n", c=KC),
                                                f32(hT[0][:, :, cols]), ALU.subtract)
                    elif n < KEY:
                        for m in range(2):
                            cols = slice((2 * (n - CTX) + m) * P, (2 * (n - CTX) + m + 1) * P)
                            ins = dve.tensor_tensor(
                                ctxT[1][:, :, cols],
                                bank[:, m * CC * P:(m + 1) * CC * P].rearrange("p (c n) -> p c n", c=CC),
                                f32(ctxT[0][:, :, cols]), ALU.subtract)
                    elif n == KEY:
                        ins = dve.tensor_tensor(kT[1][:], kf, f32(kT[0][:]), ALU.subtract)
                    elif n == VAL:
                        ins = dve.tensor_tensor(v[1][:].rearrange("p t d -> p (t d)"), bank[:],
                                                f32(v[0][:]).rearrange("p t d -> p (t d)"), ALU.subtract)
                    else:
                        dst, bias = ((xq, xbq), (xk, xbk))[n - XQ]
                        ins = dve.scalar_tensor_tensor(out=dst[1][:], in0=bank[:], scalar=bias[:], in1=f32(dst[0][:]),
                                                       op0=ALU.add, op1=ALU.subtract)
                    ins.then_inc(item_lo, 1)

                def normalise(b, h, p, j):
                    dve.wait_ge(exp_made, START + tiles_before(b, h, j + 1))
                    dve.reciprocal(rinv[:, p, j:j + 1], rsum[:, p, j:j + 1]).then_inc(rsum_inv, 1)
                    dve.wait_ge(rsum_inv, tiles_before(b, h, j + 1))
                    dve.tensor_scalar(prob[:, p, j, :], prob[:, p, j, :], rinv[:, p, j:j + 1], None, ALU.mult)\
                       .then_inc(p_normed, 1)

                def minus_max(b, h, p, j):
                    dve.wait_ge(s_mm, START + tiles_before(b, h, j + 1))
                    dve.tensor_reduce(neg_max[:, p, j:j + 1], ps_s[j % 2][:], AX.X, ALU.max, negate=True)\
                       .then_inc(max_made, 1)

                def query_lo(b, i, par):
                    dve.wait_ge(q_hi_made, START + b * H + i + 1)
                    dve.scalar_tensor_tensor(out=q[par][1][:], in0=ps_qv[:], scalar=bq[:, bass.ds(i, 1)],
                                             in1=f32(q[par][0][:]), op0=ALU.add, op1=ALU.subtract)\
                       .then_inc(q_lo_made, 1)

                def iteration(b, i, par, more):
                    for j in range(NT):
                        if j == 0 and unit_at(i - 1, more) is not None:
                            n = unit_at(i - 1, more)
                            unit_lo(dve, first_sets, ps_s[0], 0, n, ORDER[n])
                        if at_work(i, 2, H + 1):
                            h, p = i - 2, par
                            dve.wait_ge(pt_hi_made, START + tiles_before(b, h, j + 1))
                            dve.tensor_tensor(pT[p][1][:, :, j * P:(j + 1) * P],
                                              ps_t[:].rearrange("p (c n) -> p c n", c=NT),
                                              f32(pT[p][0][:, :, j * P:(j + 1) * P]), ALU.subtract)\
                               .then_inc(pt_lo_made, 1)
                        if not more and isinstance(i, int) and i == H and j == 0:
                            third_layernorm_scale(dve, 0)
                        if l3_at(i, j, more) is not None:
                            l3_lo_tile(dve, 0, l3_at(i, j, more), ps_qv)
                        if more and item_at(i, j) in range(CTX):
                            item_lo_part(b + 1, item_at(i, j), ITEM_BANK[item_at(i, j)])
                        if j == 0 and at_work(i, 2, H + 1):
                            normalise(b, i - 2, par, NT - 1)
                        if j > 0 and at_work(i, 1, H + 1):
                            normalise(b, i - 1, 1 - par, j - 1)
                        if j == 1 and at_work(i, 3, H):
                            h, p = i - 3, 1 - par
                            dve.wait_ge(at_hi_made, START + b * H + h + 1)
                            dve.tensor_tensor(at[p][1][:], ps_qv[:], f32(at[p][0][:]), ALU.subtract)\
                               .then_inc(at_lo_made, 1)
                        if j == NT - 1 and at_work(i, 0, H):
                            query_lo(b, i, par)
                        if more and item_at(i, j) in range(CTX, ITEMS):
                            item_lo_part(b + 1, item_at(i, j), ITEM_BANK[item_at(i, j)])
                        if at_work(i, 1, H + 1):
                            minus_max(b, i - 1, 1 - par, j)
                        if unit_at(i, more) is not None:
                            n = unit_at(i, more)
                            if j == 0:
                                unit_codes(dve, hn_dq, 0, n, ORDER[n])
                            elif j == 1:
                                unit_clamp(dve, hn_dq, 0, n)
                            elif j == 2:
                                unit_value(dve, hn_dq, 0, n)
                        if more and isinstance(i, int) and i == H - 2:
                            layer_norm_stats(dve, stats_index(b + 1, 1), x_tile(b + 1), (j,))
                            if j == NT - 1:
                                layer_norm_aggregate(dve, stats_index(b + 1, 1))
                    if more and isinstance(i, int) and i == H - 1:
                        dve.wait_ge(l2_mm, START + b * NT)
                        layer_norm_scale(dve, stats_index(b + 1, 1), x_tile(b + 1))

                def add_cross(b, t):
                    dve.wait_ge(xm_mm, START + b * NT + t + 1)
                    dve.tensor_tensor(x[:, b * NT + t, :], acc[t][:], x[:, b * NT + t, :], ALU.add)\
                       .then_inc(xm_added, 1)

                def third_stats(b, t, more=True):
                    dve.wait_ge(xm_added, START + b * NT + t + 1)
                    hold(dve)
                    layer_norm_stats(dve, stats_index(b, 3, more), x_tile(b), (t,))

                def second_layernorm_lo(b):
                    for t in range(NT):
                        dve.wait_ge(l2_hi, START + b * NT + t + 1)
                        dve.tensor_tensor(l2T[1][:, :, t * P:(t + 1) * P],
                                          acc[t][:].rearrange("p (c n) -> p c n", c=KC),
                                          f32(l2T[0][:, :, t * P:(t + 1) * P]), ALU.subtract).then_inc(l2_lo, 1)

                def first_heads(b, before):
                    if before:
                        second_layernorm_lo(b - 1)
                        for n in ITEMS_AFTER:
                            item_lo_part(b, n, ITEM_BANK[n], pre=False)
                    query_lo(b, 0, 0)
                    for j in range(NT):
                        if before:
                            add_cross(b - 1, j)
                            if j < NT - 1:
                                third_stats(b - 1, j)
                        if j > 0:
                            normalise(b, 0, 0, j - 1)
                        if j == NT - 1:
                            query_lo(b, 1, 1)
                            if before:
                                third_stats(b - 1, j)
                        minus_max(b, 0, 0, j)
                    if before:
                        layer_norm_aggregate(dve, stats_index(b - 1, 3))

                dve.wait_ge(x_loaded[0], 16)
                layer_norm_stats(dve, 0, x_tile(0))
                layer_norm_aggregate(dve, 0)
                layer_norm_scale(dve, 0, x_tile(0))
                dve.wait_ge(once_hi, 1)
                dve.tensor_tensor(wkv_p[1][:], wkv, f32(wkv_p[0][:]), ALU.subtract).then_inc(once_lo, 1)
                dve.wait_ge(once_hi, 2)
                dve.tensor_tensor(xwT[1].rearrange("p a c d -> p (a c d)"), ps_qv[:],
                                  f32(xwT[0].rearrange("p a c d -> p (a c d)")), ALU.subtract).then_inc(once_lo, 1)
                for n in range(ITEMS):
                    item_lo_part(0, n, acc[n] if n < CTX else ITEM_BANK[n])
                dve.wait_ge(x_loaded[1], 16 * (B - 1))
                first_heads(0, False)

                def batch(b, more):
                    pipeline(dve, b, iteration, more)
                    dve.wait_ge(bo_added, b * NT + NT)
                    for t in range(NT):
                        dve.wait_ge(acc_ready, START + b * NT + t + 1)
                        dve.tensor_tensor(x[:, b * NT + t, :], acc[t][:], x[:, b * NT + t, :], ALU.add)\
                           .then_inc(att_added, 1)
                    if more:
                        dve.wait_ge(item_mm, START + (b + 1) * ITEMS + LN1 + NT)
                    dve.wait_ge(att_added, b * NT + NT)
                    hold(dve)
                    layer_norm_stats(dve, stats_index(b, 2, more), x_tile(b))
                    layer_norm_aggregate(dve, stats_index(b, 2, more))
                    if more:
                        item_pre_part(b + 1, VALT, ITEM_BANK[VALT])
                    layer_norm_scale(dve, stats_index(b, 2, more), x_tile(b))
                    if more:
                        first_heads(b + 1, True)
                    else:
                        second_layernorm_lo(b)
                        third_layernorm_scale(dve, 1)
                        for t in range(NT):
                            add_cross(b, t)
                            if t < NT - 1:
                                third_stats(b, t, False)

                batches(dve, batch)

        with ExitStack() as ffn:
            def sb(name, shape, dt=F32):
                return ffn.enter_context(nc.sbuf_tensor(name, shape, dt))

            def pair(name, shape):
                return sb(name + "_hi", shape, F32R), sb(name + "_lo", shape, F32R)

            h3T += [pair(f"h3T{b}", [P, KC, S]) for b in range(1, B)]
            wg = [wg0, pair("wg1", [P, NCH, KC, P])]
            wu = [wu0, pair("wu1", [P, NCH, KC, P])]
            wd = [wd0, pair("wd1", [P, NCH, D])]
            inter = [pair(f"inter{n}", [P, NCH, S]) for n in range(2)]
            act_buf = [sb(f"act_buf{n}", [P, S]) for n in range(NCH)]
            dq_f = sb("dq_f", [P, 2, 512])
            dq_g = sb("dq_g", [P, 2, 512])
            dq_c = sb("dq_c", [P, 2, 512])
            dq_w = sb("dq_w", [P, 2, 512])

            dq = [[a[:, n, :] for n in range(2)] for a in (dq_f, dq_g, dq_c, dq_w)]
            sets = [(wg[n], wu[n], wd[n]) for n in range(2)]

            bank_g, bank_u = psum[0:2], psum[2:4]
            bank_d = psum[4:6]
            bank_w = psum[6:8]

            out_dram = out.rearrange("b (t p) n -> b p t n", p=P)
            GELU_A, GELU_B = 0.7978845608028654, 0.044715

            blk = ffn.enter_context(nc.Block())

            @blk.sync
            def _(sp):
                with sp.Fori(1, G) as g:
                    sp.wait_ge(dq_shift, START + g * (2 * UNITS))
                    load_codes(sp, g)
                for b in range(B - 1):
                    sp.wait_ge(down_added, 2 + (G - 1) * B * NT + (b + 1) * NT)
                    sp.dma_start(out_dram[b], x[:, b * NT:(b + 1) * NT, :]).then_inc(stored, 16)
                for t in range(NT):
                    sp.wait_ge(down_added, 2 + (G * B - 1) * NT + t + 1)
                    sp.dma_start(out_dram[B - 1][:, t, :], x[:, (B - 1) * NT + t, :]).then_inc(stored, 16)
                sp.wait_ge(stored, 16 * (B - 1 + NT))

            def units_at(b, last_group):
                made = [[] if last_group else [ORDER.index(k) for k in at] for at in UNITS_AT]
                return (made[b][0] if made[b] else None), (made[b - 1][1] if b and made[b - 1] else None)

            def units_before(b):
                return sum(u is not None for k in range(b) for u in units_at(k, False)) + \
                    (units_at(b, False)[1] is not None)

            def substeps(emit, engine):
                for b in range(B):
                    emit(0, 0, b, True, False)
                with engine.Fori(0, G // 2 - 1) as n:
                    for k in range(2 * B):
                        emit(n * 2 + (1 + k // B), 1 - k // B, k % B, False, False)
                for b in range(B):
                    emit(G - 1, 1, b, False, True)

            AHEAD = 2
            l3_bank = (bank_g[0], bank_u[0], bank_w[0], bank_w[1])

            def product_banks(g, b, n):
                return ahead_banks if isinstance(g, int) and (g, b, n) == (0, 0, 0) else (bank_g[n], bank_u[n])

            @blk.gpsimd
            def _(pool):

                layer_norm_rstd(pool, stats_index(B - 1, 3, False))

                def emit(g, gp, b, first_group, last_group):
                    if not last_group:
                        for k in UNITS_AT[b]:
                            unit_sum(pool, dq, g + 1, ORDER.index(k))
                            unit_weight(pool, dq, g + 1, ORDER.index(k), k)

                substeps(emit, pool)

            @blk.tensor
            def _(pe):
                def l3_tile(b, t, bank):
                    if b >= AHEAD:
                        pe.wait_ge(l3_lo, START + b * NT + at_least_0(t - 1))
                        pe.wait_ge(w_lo_made, START + UNITS + units_before(b - AHEAD))
                    l3_transpose(pe, b, t, bank)

                def unit(g, n, after_l3=0):
                    pe.wait_ge(w_lo_made, START + at_least_0(unit_index(g, n) - 1))
                    if after_l3:
                        pe.wait_ge(l3_lo, START + after_l3)
                    unit_transpose(pe, dq, bank_w[n % 2], g, n)

                def gate_up(g, gp, b, n):
                    s = g * B + b
                    if b == 0:
                        pe.wait_ge(w_lo_made, START + unit_index(g, 2 * (n + 1)))
                    if isinstance(g, int) and g == 0:
                        pe.wait_ge(l3_lo, START + (b + 1) * NT)
                    pe.wait_ge(v_made, START + at_least_0((s - 1) * NCH + n + 1))
                    gate_up_products(pe, sets[gp][:2], (bank_g[n], bank_u[n]), b, n)

                def down(g, gp, b, t):
                    s = g * B + b
                    if t == 0:
                        pe.wait_ge(in_lo_made, START + s * NCH + NCH)
                        if b == 0:
                            pe.wait_ge(w_lo_made, START + unit_index(g, UNITS))
                    pe.wait_ge(down_added, s * NT + t + 1)
                    i = inter[b % 2]
                    for n in range(NCH):
                        mm = mm3(pe, bank_d[t % 2][:], (i[0][:, n, t * P:(t + 1) * P], i[1][:, n, t * P:(t + 1) * P]),
                                 (wd[gp][0][:, n, :], wd[gp][1][:, n, :]), n == 0, n == NCH - 1)
                    mm.then_inc(down_mm, 1)

                for t in range(NT):
                    l3_tile(1, t, l3_bank[t])
                gate_up(0, 0, 0, 1)

                def emit(g, gp, b, first_group, last_group):
                    nb = (b + 1) % B
                    ng, ngp = (g, gp) if nb else (g + 1, 1 - gp)
                    more = nb or not last_group
                    first, second = units_at(b, last_group)
                    if more:
                        gate_up(ng, ngp, nb, 0)
                    if second is not None:
                        unit(g + 1, second)
                    ln = first_group and b + AHEAD < B
                    if more and last_group and nb == B - 1:
                        gate_up(ng, ngp, nb, 1)
                    down(g, gp, b, 0)
                    for t in range(2):
                        if ln:
                            l3_tile(b + AHEAD, t, bank_w[t])
                    down(g, gp, b, 1)
                    for t in range(2, NT):
                        if ln:
                            l3_tile(b + AHEAD, t, bank_w[t % 2])
                    if more and not (last_group and nb == B - 1):
                        gate_up(ng, ngp, nb, 1)
                    if first is not None:
                        unit(g + 1, first, (b + AHEAD + 1) * NT if ln else 0)
                    down(g, gp, b, 2)
                    down(g, gp, b, 3)

                substeps(emit, pe)

            @blk.scalar
            def _(act):
                def elementwise_sq(g, b, n):
                    e = (g * B + b) * NCH + n
                    act.wait_ge(gu_mm, e * 2 + 2)
                    act.wait_ge(in_lo_made, START + at_least_0(e - 1))
                    act.activation(act_buf[n][:], product_banks(g, b, n)[0][:], ACT.Square).then_inc(sq_made, 1)

                def elementwise_tanh(g, b, n):
                    e = (g * B + b) * NCH + n
                    act.wait_ge(z_made, e + 1)
                    act.activation(act_buf[n][:], act_buf[n][:], ACT.Tanh, scale=GELU_A * GELU_B).then_inc(tanh_made, 1)
                    act.wait_ge(v_made, START + e + 1)
                    if n == 0:
                        act.wait_ge(down_mm, START + at_least_0((g * B + b - 1) * NT))
                    act.activation(inter[b % 2][0][:, n, :], act_buf[n][:], ACT.Copy).then_inc(in_hi_made, 1)

                for n in range(NCH):
                    elementwise_sq(0, 0, n)
                    if n == 0:
                        for t in range(NT):
                            l3_hi_tile(act, 1, t, l3_bank[t])
                    elementwise_tanh(0, 0, n)

                def emit(g, gp, b, first_group, last_group):
                    nb = (b + 1) % B
                    ng = g if nb else g + 1
                    more = nb or not last_group
                    units = [] if last_group else [ORDER.index(k) for k in UNITS_AT[b]]
                    first, second = units_at(b, last_group)
                    for n, transposed in enumerate((second, first)):
                        if n < len(units):
                            unit_sign(act, dq, g + 1, units[n])
                        if more:
                            elementwise_sq(ng, nb, n)
                        if transposed is not None:
                            unit_hi(act, sets[1 - gp], bank_w[transposed % 2], g + 1, transposed, ORDER[transposed])
                        ln = first_group and b + AHEAD < B and n == 0
                        for t in range(2):
                            if ln:
                                l3_hi_tile(act, b + AHEAD, t, bank_w[t])
                        if more:
                            elementwise_tanh(ng, nb, n)
                        for t in range(2, NT):
                            if ln:
                                l3_hi_tile(act, b + AHEAD, t, bank_w[t % 2])

                substeps(emit, act)

            @blk.vector
            def _(dve):
                dve.sem_inc(down_added, 2)
                def l3_scale(b):
                    dve.wait_ge(l3_mm, START + b * NT)
                    if b < B - 1:
                        third_layernorm_scale(dve, b)
                    else:
                        layer_norm_scale(dve, stats_index(b, 3, False), x_tile(b))

                def elementwise_z(g, b, n):
                    e = (g * B + b) * NCH + n
                    dve.wait_ge(sq_made, e + 1)
                    dve.scalar_tensor_tensor(out=act_buf[n][:], in0=act_buf[n][:], scalar=1.0 / GELU_B,
                                             in1=product_banks(g, b, n)[0][:], op0=ALU.add, op1=ALU.mult)\
                       .then_inc(z_made, 1)

                def elementwise_v(g, b, n):
                    e = (g * B + b) * NCH + n
                    gate, up = product_banks(g, b, n)
                    dve.wait_ge(tanh_made, e + 1)
                    dve.scalar_tensor_tensor(out=act_buf[n][:], in0=act_buf[n][:], scalar=1.0, in1=gate[:],
                                             op0=ALU.add, op1=ALU.mult).then_inc(a_made, 1)
                    dve.wait_ge(a_made, e + 1)
                    dve.scalar_tensor_tensor(out=act_buf[n][:], in0=act_buf[n][:], scalar=0.5, in1=up[:],
                                             op0=ALU.mult, op1=ALU.mult).then_inc(v_made, 1)

                def elementwise_lo(g, b, n):
                    e = (g * B + b) * NCH + n
                    dve.wait_ge(in_hi_made, e + 1)
                    i = inter[b % 2]
                    dve.tensor_tensor(i[1][:, n, :], act_buf[n][:], f32(i[0][:, n, :]), ALU.subtract)\
                       .then_inc(in_lo_made, 1)

                def add_down(g, b, t):
                    s = g * B + b
                    dve.wait_ge(down_mm, START + s * NT + t + 1)
                    xt = x[:, b * NT + t, :]
                    dve.tensor_tensor(xt, bank_d[t % 2][:], xt, ALU.add).then_inc(down_added, 1)

                for n in range(NCH):
                    elementwise_z(0, 0, n)
                    if n == 0:
                        for t in range(NT):
                            l3_lo_tile(dve, 1, t, l3_bank[t])
                        layer_norm_stats(dve, stats_index(B - 1, 3, False), x_tile(B - 1), (NT - 1,))
                        layer_norm_aggregate(dve, stats_index(B - 1, 3, False))
                    elementwise_v(0, 0, n)
                    elementwise_lo(0, 0, n)

                def emit(g, gp, b, first_group, last_group):
                    nb = (b + 1) % B
                    ng = g if nb else g + 1
                    more = nb or not last_group
                    units = [] if last_group else [ORDER.index(k) for k in UNITS_AT[b]]
                    first, second = units_at(b, last_group)
                    for n, transposed in enumerate((second, first)):
                        ln = first_group and b + AHEAD < B and n == 0
                        if n < len(units):
                            unit_codes(dve, dq, g + 1, units[n], ORDER[units[n]])
                        if ln:
                            l3_scale(b + AHEAD)
                        if more and not (last_group and nb == B - 1 and n == 1):
                            elementwise_z(ng, nb, n)
                        if transposed is not None:
                            unit_lo(dve, sets[1 - gp], bank_w[transposed % 2], g + 1, transposed, ORDER[transposed])
                        for t in range(2):
                            if ln:
                                l3_lo_tile(dve, b + AHEAD, t, bank_w[t])
                        if n < len(units):
                            unit_clamp(dve, dq, g + 1, units[n])
                        if more:
                            elementwise_v(ng, nb, n)
                        if n < len(units):
                            unit_value(dve, dq, g + 1, units[n])
                        if more:
                            elementwise_lo(ng, nb, n)
                        if last_group and nb == B - 1 and n == 0:
                            elementwise_z(ng, nb, 1)
                        for t in range(2, NT):
                            if ln:
                                l3_lo_tile(dve, b + AHEAD, t, bank_w[t % 2])
                        add_down(g, b, 2 * n)
                        add_down(g, b, 2 * n + 1)

                substeps(emit, dve)


_INS = ['x', 'ctx_1024', 'L0_attn_Wq', 'L0_attn_bq', 'L0_attn_Wk', 'L0_attn_bk', 'L0_attn_Wv', 'L0_attn_bv',
        'L0_attn_Wo', 'L0_attn_bo', 'L0_xattn_Wq', 'L0_xattn_bq', 'L0_xattn_Wk', 'L0_xattn_bk',
        'L0_ffn_gate_W_packed', 'L0_ffn_gate_scales', 'L0_ffn_up_W_packed', 'L0_ffn_up_scales',
        'L0_ffn_down_W_packed', 'L0_ffn_down_scales']


def kernel(**inputs):
    import numpy as _np
    import concourse.bacc as _bacc
    from concourse import mybir as _mybir
    from concourse.bass_utils import run_bass_kernel_spmd as _run

    nc = _bacc.Bacc("TRN2", target_bir_lowering=False, num_devices=1)
    arrays, args = {}, []
    for name in _INS:
        a = _np.ascontiguousarray(inputs[name])
        arrays[f"in_{name}_dram"] = a
        args.append(nc.dram_tensor(f"in_{name}_dram", a.shape, _mybir.dt.from_np(a.dtype), kind="ExternalInput").ap())
    out = nc.dram_tensor("out_0_dram", inputs["x"].shape, _mybir.dt.float32, kind="ExternalOutput").ap()
    decoder_layer(nc, *args, out)
    r = _run(nc, [arrays], core_ids=[0])
    return r.results[0]["out_0_dram"]
```
